# Optimizing a Trainium2 kernel written in Bass

```python
import numpy as np
import jax
import jax.numpy as jnp

def _softmax(x, axis=-1):
    return jax.nn.softmax(x, axis=axis)

def _gelu(x):
    return jax.nn.gelu(x, approximate=True)

def _silu(x):
    return jax.nn.silu(x)

def _sigmoid(x):
    return jax.nn.sigmoid(x)

def _layernorm(x, axis=-1, eps=1e-05):
    m = jnp.mean(x, axis=axis, keepdims=True)
    v = jnp.var(x, axis=axis, keepdims=True)
    return (x - m) / jnp.sqrt(v + eps)

def _scatter_add(tgt, idx, src, axis=0):
    return tgt.at[idx].add(src)

def _segment_sum(src, seg, n):
    return jax.ops.segment_sum(src, seg, n)
kernel_name = 'mk_gnn_preln_d2_gnn_r8_9d7b7c'

def setup_inputs(seed: int=0):
    np.random.seed(seed)
    _w = jnp.asarray

    def _rec_inputs():
        import jax
        import jax.numpy as jnp
        _gk = jax.random.key(seed)
        x = -0.0001006 + 1 * jax.random.normal(jax.random.fold_in(_gk, 1), (6250, 96), jnp.float32)
        _s = jax.random.randint(jax.random.fold_in(_gk, 2), (50000,), 0, 6250, jnp.int32)
        _d = jax.random.randint(jax.random.fold_in(_gk, 3), (50000,), 0, 6250, jnp.int32)
        _loop = jnp.arange(6250, dtype=jnp.int32)
        src = jnp.concatenate([_s, _d, _loop])
        dst = jnp.concatenate([_d, _s, _loop])
        _o = jnp.argsort(dst, stable=True)
        src = src[_o]
        dst = dst[_o]
        edge_attr_96 = 5.93493e-05 + 1.00006 * jax.random.normal(jax.random.fold_in(_gk, 11), (106250, 96), jnp.float32)
        return (x, src, dst, edge_attr_96)
    x, src, dst, edge_attr_96 = _rec_inputs()

    def _L0_gnn_setup():
        import jax, jax.numpy as jnp
        import numpy as np
        N_NODES = 6250
        N_EDGES = 100000
        NIN = 96
        NOUT = 96
        key = jax.random.key(seed)
        ks = jax.random.split(key, 10)
        s = 1.0 / np.sqrt(NIN)
        so = 1.0 / np.sqrt(NOUT)
        return {'x': jax.random.normal(ks[0], (N_NODES, NIN), dtype=jnp.float32), 'edge_index': jax.random.randint(ks[1], (2, N_EDGES), 0, N_NODES, dtype=jnp.int64), 'edge_attr': jax.random.normal(ks[2], (N_EDGES, NIN), dtype=jnp.float32), 'W_edge': jax.random.uniform(ks[3], (NIN, NIN), jnp.float32, -s, s), 'b_edge': jax.random.uniform(ks[4], (NIN,), jnp.float32, -s, s), 'eps': jnp.zeros((), dtype=jnp.float32), 'W1': jax.random.uniform(ks[5], (NOUT, NIN), jnp.float32, -s, s), 'b1': jax.random.uniform(ks[6], (NOUT,), jnp.float32, -s, s), 'W2': jax.random.uniform(ks[7], (NOUT, NOUT), jnp.float32, -so, so), 'b2': jax.random.uniform(ks[8], (NOUT,), jnp.float32, -so, so)}
    _L0_gnn_all = _L0_gnn_setup()
    _L0_gnn_in = {k: v for k, v in _L0_gnn_all.items() if k in ('W_edge', 'b_edge', 'eps', 'W1', 'b1', 'W2', 'b2')}
    del _L0_gnn_all

    def _L1_gnn_setup():
        import jax, jax.numpy as jnp
        import numpy as np
        BN_EPS = 1e-05
        key = jax.random.key(seed)
        ks = jax.random.split(key, 5)
        N, E, D = (6250, 100000, 96)
        x = jax.random.normal(ks[0], (N, D), dtype=jnp.float32)
        edge_index = jax.random.randint(ks[1], (2, E), 0, N, dtype=jnp.int64)
        Wl = jax.random.normal(ks[2], (D, D), dtype=jnp.float32) / np.sqrt(D)
        bl = jnp.zeros((D,), dtype=jnp.float32)
        Wr = jax.random.normal(ks[3], (D, D), dtype=jnp.float32) / np.sqrt(D)
        gamma = jnp.ones((D,), dtype=jnp.float32)
        beta = jnp.zeros((D,), dtype=jnp.float32)
        return {'x': x, 'edge_index': edge_index, 'Wl': Wl, 'bl': bl, 'Wr': Wr, 'gamma': gamma, 'beta': beta}
    _L1_gnn_all = _L1_gnn_setup()
    _L1_gnn_in = {k: v for k, v in _L1_gnn_all.items() if k in ('Wl', 'bl', 'Wr', 'gamma', 'beta')}
    del _L1_gnn_all
    return {'x': x, 'src': src, 'dst': dst, 'edge_attr_96': edge_attr_96, 'L0_gnn_W_edge': _L0_gnn_in['W_edge'], 'L0_gnn_b_edge': _L0_gnn_in['b_edge'], 'L0_gnn_eps': _L0_gnn_in['eps'], 'L0_gnn_W1': _L0_gnn_in['W1'], 'L0_gnn_b1': _L0_gnn_in['b1'], 'L0_gnn_W2': _L0_gnn_in['W2'], 'L0_gnn_b2': _L0_gnn_in['b2'], 'L1_gnn_Wl': _L1_gnn_in['Wl'], 'L1_gnn_bl': _L1_gnn_in['bl'], 'L1_gnn_Wr': _L1_gnn_in['Wr'], 'L1_gnn_gamma': _L1_gnn_in['gamma'], 'L1_gnn_beta': _L1_gnn_in['beta']}

def reference(x, src, dst, edge_attr_96, L0_gnn_W_edge, L0_gnn_b_edge, L0_gnn_eps, L0_gnn_W1, L0_gnn_b1, L0_gnn_W2, L0_gnn_b2, L1_gnn_Wl, L1_gnn_bl, L1_gnn_Wr, L1_gnn_gamma, L1_gnn_beta):
    import jax
    import jax.numpy as jnp

    def _L0_gnn_ref(x, edge_index, edge_attr, W_edge, b_edge, eps, W1, b1, W2, b2):
        import jax, jax.numpy as jnp
        import numpy as np
        N_NODES = 6250
        N_EDGES = 100000
        NIN = 96
        NOUT = 96
        ea = edge_attr @ W_edge.T + b_edge
        src, dst = (edge_index[0], edge_index[1])
        msg = jax.nn.relu(x[src] + ea)
        aggr = jax.ops.segment_sum(msg, dst, num_segments=N_NODES)
        h = (1.0 + eps) * x + aggr
        h = jax.nn.relu(h @ W1.T + b1)
        return h @ W2.T + b2

    def _L1_gnn_ref(x, edge_index, Wl, bl, Wr, gamma, beta):
        import jax, jax.numpy as jnp
        import numpy as np
        BN_EPS = 1e-05
        N = x.shape[0]
        src, dst = (edge_index[0], edge_index[1])
        msg_sum = jax.ops.segment_sum(x[src], dst, num_segments=N)
        deg = jax.ops.segment_sum(jnp.ones_like(src, dtype=x.dtype), dst, num_segments=N)
        neigh_mean = msg_sum / jnp.maximum(deg, 1.0)[:, None]
        h = jnp.einsum('nd,od->no', neigh_mean, Wl) + bl + jnp.einsum('nd,od->no', x, Wr)
        mu = h.mean(axis=0)
        var = h.var(axis=0)
        h = (h - mu) * jax.lax.rsqrt(var + BN_EPS) * gamma + beta
        return jax.nn.relu(h)
    edge_index = jnp.stack([src, dst])
    h = jnp.maximum(_layernorm(x, axis=-1), 0.0)
    x = x + _L0_gnn_ref(h, edge_index, edge_attr_96, L0_gnn_W_edge, L0_gnn_b_edge, L0_gnn_eps, L0_gnn_W1, L0_gnn_b1, L0_gnn_W2, L0_gnn_b2)
    h = jnp.maximum(_layernorm(x, axis=-1), 0.0)
    x = x + _L1_gnn_ref(h, edge_index, L1_gnn_Wl, L1_gnn_bl, L1_gnn_Wr, L1_gnn_gamma, L1_gnn_beta)
    return x

_drawn_inputs = setup_inputs


def setup_inputs(seed=0):
    import zlib

    import numpy as np

    out = dict(_drawn_inputs(seed))
    spreads = {'L1_gnn_bl': (0.0, 0.8), 'L1_gnn_gamma': (1.0, 0.2), 'L1_gnn_beta': (0.0, 0.1)}
    factors = {'L0_gnn_b1': 5.966}
    for name, (base, spread) in spreads.items():
        noise = np.random.default_rng([zlib.crc32(name.encode()), seed]).standard_normal(out[name].shape)
        drawn = base * np.exp(spread * noise) if base else spread * noise
        out[name] = jnp.asarray(drawn.astype(out[name].dtype))
    for name, factor in factors.items():
        out[name] = (out[name] * factor).astype(out[name].dtype)
    return out
```

```python
from contextlib import ExitStack

import numpy as np
import concourse.bass as bass
from concourse import mybir

ALU = mybir.AluOpType
ACT = mybir.ActivationFunctionType
F32 = mybir.dt.float32
I32 = mybir.dt.int32

NODES, D, EDGES = 6250, 96, 106250
NP, NT = 125, 50
SPLIT = 120
LANES, TPG = 128, 4
GE = LANES * TPG
SLOTS = 8
HALF = SLOTS // 2
STEPS = -(-EDGES // (GE * SLOTS))
GROUPS = STEPS * SLOTS
EPAD = GROUPS * GE
WIN = 64
GWIN = 512
GWINS = -(-NODES // GWIN)
SUMS = GWINS * GWIN
LN_EPS = BN_EPS = 1e-5
NO_NODE = 1 << 20

W_EDGE, W_1, W_2, W_L, W_R = (D * i for i in range(5))
C_B1, C_BL, C_GAMMA, C_BETA, C_EPS = (5 * D + i for i in range(5))
W_COLS = 5 * D + 5

TCH = 4
CHUNKS = [(t, min(TCH, NT - t)) for t in range(0, NT, TCH)]
NCH = len(CHUNKS)


def graph_layers(nc, x, edge_attr_t, src_blocks, dst_cols, dst_first, weights, ident_in, out):
    h_dram = nc.dram_tensor("h_rows", [NODES, D], F32).ap()
    h2_dram = nc.dram_tensor("h2_rows", [NODES, D], F32).ap()

    with ExitStack() as ctx:
        def sb(name, shape, dt=F32):
            return ctx.enter_context(nc.sbuf_tensor(name, shape, dt))

        def sem(name):
            return ctx.enter_context(nc.semaphore(name))

        x_nm = sb("x_nm", [NP, NT * D])
        h_nm = sb("h_nm", [NP, NT * D])
        sums = sb("sums", [D + 1, SUMS])
        h2_fm = sb("h2_fm", [D, NT * NP])
        rdeg = sb("rdeg", [D, NT * NP])
        w = sb("w", [D + 1, W_COLS])
        ident = sb("ident", [LANES, LANES])
        ones = sb("ones", [LANES, LANES])
        iota = sb("iota", [LANES, GWIN])
        dst_i = sb("dst_i", [LANES, GROUPS * TPG], I32)
        rel = sb("rel", [LANES, GROUPS * TPG])
        base_i = sb("base_i", [LANES, GROUPS], I32)
        idx = sb("idx", [LANES, 2, HALF * TPG], I32)
        attr = sb("attr", [D + 1, HALF, 2 * GE])
        gat = sb("gat", [LANES, SLOTS, TPG * D])
        pre = sb("pre", [LANES, 2, TPG * D])
        msg = sb("msg", [LANES, 2, TPG * (D + 1)])
        sel = sb("sel", [LANES, 2, TPG * WIN])
        gsel = sb("gsel", [LANES, TPG * GWIN])
        bounds = sb("bounds", [LANES, 8])
        wide_i = sb("wide_i", [1, 1], I32)
        stats = sb("stats", [NP, NT, 6])
        mv = sb("mv", [NP, NT, 2])
        sd = sb("sd", [NP, NT])
        rstd = sb("rstd", [NP, NT])
        nmr = sb("nmr", [NP, NT])
        u = sb("u", [D, 2, TCH * NP])
        z = sb("z", [D + 1, 2, TCH * NP])
        epsln = sb("epsln", [LANES, 1])
        eps1 = sb("eps1", [D + 1, 1])
        bstats = sb("bstats", [D, NCH, 6])
        bmv = sb("bmv", [D, 2])
        bn = sb("bn", [D, 6])

        banks = [ctx.enter_context(nc.psum_tensor(f"bank{i}", [LANES, 512], F32)) for i in range(8)]
        ea_ps, agg_ps, t_ps, z_ps = banks[0:2], banks[2:4], banks[4:6], banks[6:8]
        y_ps = ea_ps

        def nodes_of(rows, t0, nt):
            return rows.rearrange("(p t) f -> p (t f)", t=NT)[:, t0 * D:(t0 + nt) * D]

        def sums_of(t0, nt):
            return sums[:, 0:NODES].rearrange("f (p t) -> f t p", t=NT)[:, t0:t0 + nt, :]

        def tiles(ap, nt, n=NP):
            return ap.rearrange("f (t p) -> f t p", t=nt, p=n)

        rel3 = rel[:, :].rearrange("p (g k) -> p g k", k=TPG)

        x_in, w_in, dst_in = sem("x_in"), sem("w_in"), sem("dst_in")
        consts_set = sem("consts_set")
        ones_set = sem("ones_set")
        rel_step = sem("rel_step")
        bad_summed, wide_ready = sem("bad_summed"), sem("wide_ready")
        mv_done, sd_done, scale_done = sem("mv_done"), sem("sd_done"), sem("scale_done")
        bn_step = sem("bn_step")
        h_done, h_out = sem("h_done"), sem("h_out")
        mv2_done, sd2_done, scale2_done = sem("mv2_done"), sem("sd2_done"), sem("scale2_done")
        h2_done, h2_out = sem("h2_done"), sem("h2_out")
        t_done, u_done, z_mm, z_done, y_mm, x1_done = (
            sem(n) for n in ("t_done", "u_done", "z_mm", "z_done", "y_mm", "x1_done"))
        sums_cleared = sem("sums_cleared")
        t2_done, t2_used, deg_mm, rdeg_max, rdeg_done = (
            sem(n) for n in ("t2_done", "t2_used", "deg_mm", "rdeg_max", "rdeg_done"))
        mean_done, l1_mm, l1_done, bstat_done = (
            sem(n) for n in ("mean_done", "l1_mm", "l1_done", "bstat_done"))
        bmv_done, bsd_done, affine_done = sem("bmv_done"), sem("bsd_done"), sem("affine_done")
        y1_done, y1_t, out_done, stored = sem("y1_done"), sem("y1_t"), sem("out_done"), sem("stored")
        dve_step = sem("dve_step")
        slot_taken = sem("slot_taken")

        idx_in = [[sem(f"idx_in{p}_{h}") for h in range(2)] for p in range(2)]
        gathered = [[sem(f"gathered{p}_{s}") for s in range(SLOTS)] for p in range(2)]
        attr_in = [sem(f"attr_in{q}") for q in range(HALF)]
        ea_done, pre_done, msg_done = sem("ea_done"), sem("pre_done"), sem("msg_done")
        sel_done = [sem(f"sel_done{p}") for p in range(2)]
        agg_done = [sem(f"agg_done{p}") for p in range(2)]
        acc_done = [sem(f"acc_done{p}") for p in range(2)]
        gsel_done = [sem(f"gsel_done{p}") for p in range(2)]
        gagg_done = [sem(f"gagg_done{p}") for p in range(2)]
        gacc_done = [sem(f"gacc_done{p}") for p in range(2)]

        def edge_loop(eng, body):
            body(0)
            with eng.Fori(1, STEPS) as i:
                body(i)

        def wait_past(eng, s, i, count):
            if not isinstance(i, int) or count > 0:
                eng.wait_ge(s, count)

        block = ctx.enter_context(nc.Block())

        @block.sync
        def _(sp):
            for a, b in ((0, SPLIT), (SPLIT, NP)):
                sp.dma_start(x_nm[a:b, :], nodes_of(x, 0, NT)[a:b, :]).then_inc(x_in, 16)
            sp.dma_start(w[:, :], weights[:, :]).then_inc(w_in, 16)
            sp.dma_start(ident[:, :], ident_in[:, :]).then_inc(w_in, 16)
            sp.dma_start(dst_i[:, :], dst_cols[:, :]).then_inc(dst_in, 16)
            sp.dma_start(base_i[:, :], dst_first.to_broadcast([LANES, GROUPS])).then_inc(dst_in, 16)

            def load_idx(p, i, h):
                for s in range(h * HALF, (h + 1) * HALF):
                    if p == 1:
                        wait_past(sp, gathered[1][s], i, i * 16 * TPG)
                        if isinstance(i, int):
                            sp.wait_ge(gathered[0][s], STEPS * 16 * TPG)
                    else:
                        wait_past(sp, gathered[0][s], i, i * 16 * TPG)
                row = i * 2 + h
                src = src_blocks[row] if isinstance(i, int) else \
                    src_blocks[bass.ds(row, 1)].rearrange("a p k -> (a p) k")
                sp.dma_start(idx[:, h, :], src).then_inc(idx_in[p][h], 16)

            def pass0(i):
                for q in range(HALF):
                    if q % 2 == 0:
                        load_idx(0, i, q // 2)
                    wait_past(sp, ea_done, i, (i - 1) * SLOTS + 2 * q + 2)
                    sp.dma_start(attr[0:D, q, :],
                                 edge_attr_t[:, bass.ds(i * (SLOTS * GE) + q * 2 * GE, 2 * GE)]
                                 ).then_inc(attr_in[q], 16)

            pass0(0)
            for c in range(NT // 10):
                sp.wait_ge(h_done, 10 * (c + 1))
                for a, b in ((0, SPLIT), (SPLIT, NP)):
                    sp.dma_start(nodes_of(h_dram, c * 10, 10)[a:b, :],
                                 h_nm[a:b, c * 10 * D:(c + 1) * 10 * D]).then_inc(h_out, 16)
            with sp.Fori(1, STEPS) as i:
                pass0(i)

            for h in range(2):
                load_idx(1, 0, h)
            for t0, nt in CHUNKS:
                sp.wait_ge(h2_done, t0 + nt)
                for a, b in ((0, SPLIT), (SPLIT, NP)):
                    sp.dma_start(nodes_of(h2_dram, t0, nt)[a:b, :],
                                 h_nm[a:b, t0 * D:(t0 + nt) * D]).then_inc(h2_out, 16)
            with sp.Fori(1, STEPS) as i:
                for h in range(2):
                    load_idx(1, i, h)

            for c, (t0, nt) in enumerate(CHUNKS):
                sp.wait_ge(out_done, c + 1)
                for a, b in ((0, SPLIT), (SPLIT, NP)):
                    sp.dma_start(nodes_of(out, t0, nt)[a:b, :],
                                 x_nm[a:b, t0 * D:(t0 + nt) * D]).then_inc(stored, 16)
            sp.wait_ge(stored, 32 * NCH)

        @block.gpsimd
        def _(pool):
            nc.gpsimd.iota(iota[:, :], pattern=[[1, GWIN]], base=0, channel_multiplier=0,
                           allow_small_or_imprecise_dtypes=True).then_inc(consts_set, 1)
            nc.gpsimd.memset(sums[:, :], 0.0).then_inc(consts_set, 1)

            def gathers(p, i, table):
                for s in range(SLOTS):
                    if s % HALF == 0:
                        pool.wait_ge(idx_in[p][s // HALF], 16 * (i + 1))
                    wait_past(pool, pre_done if p == 0 else agg_done[1], i, (i - 1) * SLOTS + s + 1)
                    pool.sem_inc(slot_taken, 1)
                    for k in range(TPG):
                        col = (s % HALF) * TPG + k
                        nc.gpsimd.indirect_dma_start(
                            out=gat[:, s, k * D:(k + 1) * D], out_offset=None, in_=table[:, :],
                            in_offset=bass.IndirectOffsetOnAxis(ap=idx[:, s // HALF, col:col + 1], axis=0),
                        ).then_inc(gathered[p][s], 16)

            pool.wait_ge(h_out, 32 * (NT // 10))
            edge_loop(pool, lambda i: gathers(0, i, h_dram))

            pool.wait_ge(u_done, NCH)
            nc.gpsimd.memset(sums[0:D, :], 0.0).then_inc(sums_cleared, 1)
            pool.wait_ge(h2_out, 32 * NCH)
            edge_loop(pool, lambda i: gathers(1, i, h2_dram))

        @block.tensor
        def _(pe):
            pe.wait_ge(w_in, 32)
            pe.wait_ge(ones_set, 3)
            pe.wait_ge(rel_step, 7)
            nc.tensor.matmul(t_ps[0][0:1, 0:1], bounds[:, 6:7], ones[:, 0:1],
                             start=True, stop=True).then_inc(bad_summed, 1)
            pe.wait_ge(wide_ready, 1)
            wide = pe.value_load(wide_i[0:1, 0:1], min_val=0, max_val=LANES)

            def edge_products(i, s):
                if s % 2 == 0:
                    pe.wait_ge(attr_in[s // 2], 16 * (i + 1))
                wait_past(pe, pre_done, i, i * SLOTS + s - 1)
                for k in range(TPG):
                    a = (s % 2) * GE + k * LANES
                    mm = nc.tensor.matmul(ea_ps[s % 2][:, k * D:(k + 1) * D],
                                          attr[:, s // 2, a:a + LANES],
                                          w[:, W_EDGE:W_EDGE + D], start=True, stop=True)
                mm.then_inc(ea_done, 1)

            def messages(p, s, k):
                if p == 0:
                    return msg[:, s % 2, k * (D + 1):(k + 1) * (D + 1)]
                return gat[:, s, k * D:(k + 1) * D]

            def messages_ready(p, i, s):
                if p == 0:
                    pe.wait_ge(msg_done, i * SLOTS + s + 1)
                else:
                    pe.wait_ge(gathered[1][s], 16 * TPG * (i + 1))

            def sum_group(p, i, s):
                rows = D + 1 if p == 0 else D
                messages_ready(p, i, s)
                pe.wait_ge(sel_done[p], i * SLOTS + s + 1)
                wait_past(pe, acc_done[p], i, i * SLOTS + s - 1)
                for k in range(TPG):
                    mm = nc.tensor.matmul(agg_ps[s % 2][0:rows, 0:WIN], messages(p, s, k),
                                          sel[:, s % 2, k * WIN:(k + 1) * WIN],
                                          start=(k == 0), stop=(k == TPG - 1))
                mm.then_inc(agg_done[p], 1)

            def sum_group_general(p, i, s):
                rows = D + 1 if p == 0 else D
                messages_ready(p, i, s)
                for v in range(GWINS):
                    n = (i * SLOTS + s) * GWINS + v
                    pe.wait_ge(gsel_done[p], n + 1)
                    wait_past(pe, gacc_done[p], i, n)
                    for k in range(TPG):
                        mm = nc.tensor.matmul(agg_ps[0][0:rows, :], messages(p, s, k),
                                              gsel[:, k * GWIN:(k + 1) * GWIN],
                                              start=(k == 0), stop=(k == TPG - 1))
                    mm.then_inc(gagg_done[p], 1)
                pe.wait_ge(gacc_done[p], (i * SLOTS + s + 1) * GWINS)
                pe.nop().then_inc(agg_done[p], 1)

            def pass_narrow(p):
                def turn(i):
                    for s in range(SLOTS):
                        if p == 0:
                            edge_products(i, s)
                        sum_group(p, i, s)
                edge_loop(pe, turn)

            def pass_wide(p):
                def turn(i):
                    for s in range(SLOTS):
                        if p == 0:
                            edge_products(i, s)
                        sum_group_general(p, i, s)
                edge_loop(pe, turn)

            def either(p):
                with pe.If(wide < 1):
                    pass_narrow(p)
                with pe.Else():
                    pass_wide(p)

            either(0)

            def turn_h(c):
                t0, nt = CHUNKS[c]
                if c == 0:
                    pe.wait_ge(h_done, NT)
                if c >= 2:
                    pe.wait_ge(u_done, c - 1)
                for j in range(nt):
                    mm = nc.tensor.transpose(t_ps[c % 2][0:D, j * NP:(j + 1) * NP],
                                             h_nm[:, (t0 + j) * D:(t0 + j + 1) * D], ident[0:NP, 0:NP])
                mm.then_inc(t_done, 1)

            def first_product(c):
                t0, nt = CHUNKS[c]
                pe.wait_ge(u_done, c + 1)
                if c >= 2:
                    pe.wait_ge(z_done, c - 1)
                nc.tensor.matmul(z_ps[c % 2][0:D, 0:nt * NP], w[0:D, W_1:W_1 + D],
                                 u[:, c % 2, 0:nt * NP], start=True, stop=True).then_inc(z_mm, 1)

            def second_product(c):
                t0, nt = CHUNKS[c]
                pe.wait_ge(z_done, c + 1)
                if c >= 2:
                    pe.wait_ge(x1_done, c - 1)
                for j in range(nt):
                    mm = nc.tensor.matmul(y_ps[c % 2][0:NP, j * D:(j + 1) * D],
                                          z[:, c % 2, j * NP:(j + 1) * NP],
                                          w[:, W_2:W_2 + D], start=True, stop=True)
                mm.then_inc(y_mm, 1)

            for c in range(NCH + 2):
                if c < NCH:
                    turn_h(c)
                if 1 <= c <= NCH:
                    first_product(c - 1)
                if c >= 2:
                    second_product(c - 2)

            for c, (t0, nt) in enumerate(CHUNKS):
                pe.wait_ge(h2_done, t0 + nt)
                if c >= 2:
                    pe.wait_ge(t2_used, c - 1)
                else:
                    pe.wait_ge(u_done, NCH)
                for j in range(nt):
                    mm = nc.tensor.transpose(t_ps[c % 2][0:D, j * NP:(j + 1) * NP],
                                             h_nm[:, (t0 + j) * D:(t0 + j + 1) * D], ident[0:NP, 0:NP])
                mm.then_inc(t2_done, 1)
                if c >= 2:
                    pe.wait_ge(rdeg_max, c - 1)
                else:
                    pe.wait_ge(z_done, NCH)
                nc.tensor.matmul(tiles(z_ps[c % 2][0:D, 0:nt * NP], nt), ones[D:D + 1, 0:D],
                                 sums_of(t0, nt)[D:D + 1], start=True, stop=True).then_inc(deg_mm, 1)

            either(1)

            for c, (t0, nt) in enumerate(CHUNKS):
                if c >= 2:
                    pe.wait_ge(l1_done, c - 1)
                else:
                    pe.wait_ge(rdeg_max, NCH)
                    pe.wait_ge(t2_used, NCH)
                nc.tensor.matmul(z_ps[c % 2][0:D, 0:nt * NP], w[0:D, W_R:W_R + D],
                                 h2_fm[:, t0 * NP:(t0 + nt) * NP], start=True, stop=False)
                pe.wait_ge(mean_done, c + 1)
                nc.tensor.matmul(z_ps[c % 2][0:D, 0:nt * NP], w[0:D, W_L:W_L + D],
                                 u[:, c % 2, 0:nt * NP], start=False, stop=True).then_inc(l1_mm, 1)
            for c, (t0, nt) in enumerate(CHUNKS):
                pe.wait_ge(y1_done, c + 1)
                if c >= 2:
                    pe.wait_ge(out_done, c - 1)
                for j in range(nt):
                    mm = nc.tensor.transpose(y_ps[c % 2][0:NP, j * D:(j + 1) * D],
                                             h2_fm[:, (t0 + j) * NP:(t0 + j + 1) * NP], ident[0:D, 0:D])
                mm.then_inc(y1_t, 1)

        @block.scalar
        def _(act):
            def norm_tiles(scale_ready, h_ready):
                def tile(t):
                    nc.scalar.activation(h_nm[:, t * D:(t + 1) * D], x_nm[:, t * D:(t + 1) * D], ACT.Relu,
                                         bias=nmr[:, t:t + 1], scale=rstd[:, t:t + 1]).then_inc(h_ready, 1)
                return tile

            tile0 = norm_tiles(scale_done, h_done)
            for c in range(NT // 10):
                act.wait_ge(mv_done, c + 1)
                if c == 0:
                    act.wait_ge(ones_set, 5)
                nc.scalar.activation(sd[:, c * 10:(c + 1) * 10], mv[:, c * 10:(c + 1) * 10, 1], ACT.Sqrt,
                                     bias=epsln[0:NP, :]).then_inc(sd_done, 1)
                act.wait_ge(scale_done, c + 1)
                for t in range(c * 10, (c + 1) * 10):
                    tile0(t)

            def relu_messages(i):
                for s in range(SLOTS):
                    act.wait_ge(pre_done, i * SLOTS + s + 1)
                    wait_past(act, agg_done[0], i, i * SLOTS + s - 1)
                    nc.scalar.activation(
                        msg[:, s % 2, :].rearrange("p (k f) -> p k f", f=D + 1)[:, :, 0:D],
                        pre[:, s % 2, :].rearrange("p (k f) -> p k f", f=D), ACT.Relu).then_inc(msg_done, 1)

            act.wait_ge(ones_set, 5)
            edge_loop(act, relu_messages)

            tile1 = norm_tiles(scale2_done, h2_done)

            def relu_z(c):
                t0, nt = CHUNKS[c]
                act.wait_ge(z_mm, c + 1)
                if c >= 2:
                    act.wait_ge(y_mm, c - 1)
                nc.scalar.activation(z[0:D, c % 2, 0:nt * NP], z_ps[c % 2][0:D, 0:nt * NP], ACT.Relu,
                                     bias=w[0:D, C_B1:C_B1 + 1]).then_inc(z_done, 1)

            def norm_h2(c):
                t0, nt = CHUNKS[c]
                act.wait_ge(mv2_done, c + 1)
                nc.scalar.activation(sd[:, t0:t0 + nt], mv[:, t0:t0 + nt, 1], ACT.Sqrt,
                                     bias=epsln[0:NP, :]).then_inc(sd2_done, 1)
                act.wait_ge(scale2_done, c + 1)
                act.wait_ge(t_done, c + 1)
                if c == 0:
                    act.wait_ge(h_out, 32 * (NT // 10))
                for t in range(t0, t0 + nt):
                    tile1(t)

            for c in range(NCH + 1):
                if c < NCH:
                    relu_z(c)
                if c >= 3:
                    norm_h2(c - 3)
            for c in range(NCH - 2, NCH):
                norm_h2(c)
            for c, (t0, nt) in enumerate(CHUNKS):
                act.wait_ge(t2_done, c + 1)
                nc.scalar.activation(h2_fm[:, t0 * NP:(t0 + nt) * NP], t_ps[c % 2][0:D, 0:nt * NP],
                                     ACT.Identity).then_inc(t2_used, 1)

            for c, (t0, nt) in enumerate(CHUNKS):
                act.wait_ge(l1_mm, c + 1)
                nc.scalar.activation(h2_fm[:, t0 * NP:(t0 + nt) * NP], z_ps[c % 2][0:D, 0:nt * NP],
                                     ACT.Identity, bias=w[0:D, C_BL:C_BL + 1]).then_inc(l1_done, 1)
            act.wait_ge(bmv_done, 1)
            nc.scalar.activation(bn[:, 0:1], bmv[:, 1:2], ACT.Sqrt, bias=epsln[0:D, :]).then_inc(bsd_done, 1)
            act.wait_ge(affine_done, 1)
            for c, (t0, nt) in enumerate(CHUNKS):
                nc.scalar.activation(h2_fm[:, t0 * NP:(t0 + nt) * NP], h2_fm[:, t0 * NP:(t0 + nt) * NP],
                                     ACT.Relu, bias=bn[:, 4:5], scale=bn[:, 2:3]).then_inc(y1_done, 1)

        @block.vector
        def _(dve):
            steps = [0]

            def in_order(ins):
                steps[0] += 1
                ins.then_inc(dve_step, 1)
                dve.wait_ge(dve_step, steps[0])

            nc.vector.memset(ones[:, :], 1.0).then_inc(ones_set, 1)
            nc.vector.memset(attr[D:D + 1, :, :], 1.0).then_inc(ones_set, 1)
            nc.vector.memset(z[D:D + 1, :, :], 1.0).then_inc(ones_set, 1)
            nc.vector.memset(msg[:, :, :], 1.0).then_inc(ones_set, 1)
            nc.vector.memset(epsln[:, :], LN_EPS).then_inc(ones_set, 1)

            dve.wait_ge(dst_in, 32)
            nc.vector.tensor_tensor(rel3, dst_i[:, :].rearrange("p (g k) -> p g k", k=TPG),
                                    base_i[:, :].unsqueeze(2).to_broadcast([LANES, GROUPS, TPG]),
                                    ALU.subtract).then_inc(rel_step, 1)
            full, part = EDGES // LANES, EDGES % LANES
            dve.wait_ge(rel_step, 1)
            nc.vector.tensor_reduce(bounds[:, 0:1], rel[:, 0:full], mybir.AxisListType.X,
                                    ALU.max).then_inc(rel_step, 1)
            nc.vector.tensor_reduce(bounds[:, 1:2], rel[:, 0:full], mybir.AxisListType.X,
                                    ALU.min).then_inc(rel_step, 1)
            dve.wait_ge(rel_step, 3)
            nc.vector.tensor_tensor(bounds[0:part, 0:1], bounds[0:part, 0:1], rel[0:part, full:full + 1],
                                    ALU.max).then_inc(rel_step, 1)
            nc.vector.tensor_tensor(bounds[0:part, 1:2], bounds[0:part, 1:2], rel[0:part, full:full + 1],
                                    ALU.min).then_inc(rel_step, 1)
            dve.wait_ge(rel_step, 5)
            nc.vector.tensor_scalar(bounds[:, 2:3], bounds[:, 1:2], 0.0, None, ALU.is_lt).then_inc(rel_step, 1)
            dve.wait_ge(rel_step, 6)
            nc.vector.scalar_tensor_tensor(out=bounds[:, 6:7], in0=bounds[:, 0:1], scalar=float(WIN),
                                           in1=bounds[:, 2:3], op0=ALU.is_ge, op1=ALU.max
                                           ).then_inc(rel_step, 1)
            dve.wait_ge(bad_summed, 1)
            nc.vector.tensor_copy(wide_i[0:1, 0:1], t_ps[0][0:1, 0:1]).then_inc(wide_ready, 1)

            def norm_scales(t0, nt, sds, n, ready):
                dve.wait_ge(sds, n)
                in_order(nc.vector.reciprocal(rstd[:, t0:t0 + nt], sd[:, t0:t0 + nt]))
                nc.vector.scalar_tensor_tensor(out=nmr[:, t0:t0 + nt], in0=mv[:, t0:t0 + nt, 0], scalar=-1.0,
                                               in1=rstd[:, t0:t0 + nt], op0=ALU.mult,
                                               op1=ALU.mult).then_inc(ready, 1)

            def row_stats(t0, nt, ready):
                for t in range(t0, t0 + nt):
                    ins = nc.vector.bn_stats(stats[:, t, :], x_nm[:, t * D:(t + 1) * D])
                in_order(ins)
                for t in range(t0, t0 + nt):
                    ins = nc.vector.bn_aggr(mv[:, t, :], stats[:, t, :])
                ins.then_inc(ready, 1)

            dve.wait_ge(x_in, 32)
            for c in range(NT // 10):
                row_stats(c * 10, 10, mv_done)
                if c >= 1:
                    norm_scales((c - 1) * 10, 10, sd_done, c, scale_done)
            norm_scales(NT - 10, 10, sd_done, NT // 10, scale_done)

            dve.wait_ge(wide_ready, 1)
            wide = dve.value_load(wide_i[0:1, 0:1], min_val=0, max_val=LANES)
            dve.wait_ge(consts_set, 2)

            def add_gathered(i, s):
                dve.wait_ge(ea_done, i * SLOTS + s + 1)
                dve.wait_ge(gathered[0][s], 16 * TPG * (i + 1))
                wait_past(dve, msg_done, i, i * SLOTS + s - 1)
                nc.vector.tensor_tensor(pre[:, s % 2, :], ea_ps[s % 2][:, 0:TPG * D], gat[:, s, :],
                                        ALU.add).then_inc(pre_done, 1)

            def select(p, i, s):
                wait_past(dve, agg_done[p], i, i * SLOTS + s - 1)
                g = i * SLOTS + s
                r = rel3[:, g:g + 1, :] if isinstance(i, int) else rel3[:, bass.ds(g, 1), :]
                nc.vector.tensor_tensor(
                    sel[:, s % 2, :].rearrange("p (k n) -> p k n", n=WIN),
                    iota[:, 0:WIN].unsqueeze(1).to_broadcast([LANES, TPG, WIN]),
                    r.rearrange("p a k -> p (a k)").unsqueeze(2).to_broadcast([LANES, TPG, WIN]),
                    ALU.is_equal).then_inc(sel_done[p], 1)

            def accumulate(p, g):
                rows = D + 1 if p == 0 else D
                dve.wait_ge(agg_done[p], g + 1)
                b = base_i[0:1, g:g + 1] if isinstance(g, int) else base_i[0:1, bass.ds(g, 1)]
                at = dve.value_load(b, min_val=0, max_val=NODES - 1)
                window = sums[0:rows, bass.ds(at, WIN)]
                dve.wait_ge(acc_done[p], g)
                return window

            def pass_narrow(p):
                rows = D + 1 if p == 0 else D

                def add_group(i, s):
                    g = i * SLOTS + s
                    window = accumulate(p, g)
                    nc.vector.tensor_tensor(window, window, agg_ps[s % 2][0:rows, 0:WIN],
                                            ALU.add).then_inc(acc_done[p], 1)

                def turn(i):
                    for s in range(SLOTS):
                        select(p, i, s)
                        if p == 0:
                            add_gathered(i, s)
                        if s > 0:
                            add_group(i, s - 1)
                    add_group(i, SLOTS - 1)
                edge_loop(dve, turn)
                dve.wait_ge(acc_done[p], GROUPS)

            def pass_wide(p):
                rows = D + 1 if p == 0 else D

                def turn(i):
                    for s in range(SLOTS):
                        if p == 0:
                            add_gathered(i, s)
                        g = i * SLOTS + s
                        r = dst_i[:, g * TPG:(g + 1) * TPG] if isinstance(i, int) else \
                            dst_i[:, bass.ds(g * TPG, TPG)]
                        for v in range(GWINS):
                            n = g * GWINS + v
                            if v > 0 or not isinstance(i, int) or s > 0:
                                dve.wait_ge(gagg_done[p], n)
                            nc.vector.scalar_tensor_tensor(
                                out=gsel[:, :].rearrange("p (k n) -> p k n", n=GWIN),
                                in0=iota[:, :].unsqueeze(1).to_broadcast([LANES, TPG, GWIN]),
                                scalar=float(v * GWIN),
                                in1=r.unsqueeze(2).to_broadcast([LANES, TPG, GWIN]),
                                op0=ALU.add, op1=ALU.is_equal).then_inc(gsel_done[p], 1)
                            dve.wait_ge(gagg_done[p], n + 1)
                            if v > 0 or not isinstance(i, int) or s > 0:
                                dve.wait_ge(gacc_done[p], n)
                            part = sums[0:rows, v * GWIN:(v + 1) * GWIN]
                            nc.vector.tensor_tensor(part, part, agg_ps[0][0:rows, :],
                                                    ALU.add).then_inc(gacc_done[p], 1)
                edge_loop(dve, turn)
                dve.wait_ge(gacc_done[p], GROUPS * GWINS)

            def either(p):
                with dve.If(wide < 1):
                    pass_narrow(p)
                with dve.Else():
                    pass_wide(p)

            either(0)

            in_order(nc.vector.tensor_scalar(eps1[:, :], w[:, C_EPS:C_EPS + 1], 1.0, None, ALU.add))

            def mix(c):
                t0, nt = CHUNKS[c]
                dve.wait_ge(t_done, c + 1)
                if c >= 2:
                    dve.wait_ge(z_mm, c - 1)
                nc.vector.scalar_tensor_tensor(
                    out=tiles(u[:, c % 2, 0:nt * NP], nt), in0=tiles(t_ps[c % 2][0:D, 0:nt * NP], nt),
                    scalar=eps1[0:D, :], in1=sums_of(t0, nt)[0:D], op0=ALU.mult, op1=ALU.add
                ).then_inc(u_done, 1)

            def residual(c):
                t0, nt = CHUNKS[c]
                dve.wait_ge(y_mm, c + 1)
                nc.vector.tensor_tensor(x_nm[:, t0 * D:(t0 + nt) * D], x_nm[:, t0 * D:(t0 + nt) * D],
                                        y_ps[c % 2][0:NP, 0:nt * D], ALU.add).then_inc(x1_done, 1)
                dve.wait_ge(x1_done, c + 1)
                row_stats(t0, nt, mv2_done)

            for c in range(NCH + 4):
                if c < NCH:
                    mix(c)
                if 2 <= c < NCH + 2:
                    residual(c - 2)
                if 3 <= c < NCH + 3:
                    t0, nt = CHUNKS[c - 3]
                    norm_scales(t0, nt, sd2_done, c - 2, scale2_done)

            for c, (t0, nt) in enumerate(CHUNKS):
                part = rdeg[:, t0 * NP:(t0 + nt) * NP]
                dve.wait_ge(deg_mm, c + 1)
                nc.vector.tensor_scalar(part, z_ps[c % 2][0:D, 0:nt * NP], 1.0, None,
                                        ALU.max).then_inc(rdeg_max, 1)
                dve.wait_ge(rdeg_max, c + 1)
                nc.vector.reciprocal(part, part).then_inc(rdeg_done, 1)

            dve.wait_ge(sums_cleared, 1)
            either(1)

            dve.wait_ge(rdeg_done, NCH)
            for c in range(NCH + 1):
                if c < NCH:
                    t0, nt = CHUNKS[c]
                    if c >= 2:
                        dve.wait_ge(l1_mm, c - 1)
                    nc.vector.tensor_tensor(
                        tiles(u[:, c % 2, 0:nt * NP], nt), sums_of(t0, nt)[0:D],
                        tiles(rdeg[:, t0 * NP:(t0 + nt) * NP], nt), ALU.mult).then_inc(mean_done, 1)
                if c >= 1:
                    t0, nt = CHUNKS[c - 1]
                    dve.wait_ge(l1_done, c)
                    nc.vector.bn_stats(bstats[:, c - 1, :],
                                       h2_fm[:, t0 * NP:(t0 + nt) * NP]).then_inc(bstat_done, 1)
            dve.wait_ge(bstat_done, NCH)
            nc.vector.bn_aggr(bmv[:, :], bstats[:, :, :].rearrange("f c s -> f (c s)")).then_inc(bmv_done, 1)
            dve.wait_ge(bsd_done, 1)
            in_order(nc.vector.reciprocal(bn[:, 1:2], bn[:, 0:1]))
            in_order(nc.vector.tensor_tensor(bn[:, 2:3], bn[:, 1:2], w[0:D, C_GAMMA:C_GAMMA + 1], ALU.mult))
            in_order(nc.vector.tensor_tensor(bn[:, 3:4], bn[:, 2:3], bmv[:, 0:1], ALU.mult))
            nc.vector.tensor_tensor(bn[:, 4:5], w[0:D, C_BETA:C_BETA + 1], bn[:, 3:4],
                                    ALU.subtract).then_inc(affine_done, 1)
            for c, (t0, nt) in enumerate(CHUNKS):
                dve.wait_ge(y1_t, c + 1)
                nc.vector.tensor_tensor(x_nm[:, t0 * D:(t0 + nt) * D], x_nm[:, t0 * D:(t0 + nt) * D],
                                        y_ps[c % 2][0:NP, 0:nt * D], ALU.add).then_inc(out_done, 1)


def kernel(x, src, dst, edge_attr_96, L0_gnn_W_edge, L0_gnn_b_edge, L0_gnn_eps, L0_gnn_W1, L0_gnn_b1,
           L0_gnn_W2, L0_gnn_b2, L1_gnn_Wl, L1_gnn_bl, L1_gnn_Wr, L1_gnn_gamma, L1_gnn_beta):
    import concourse.bacc as bacc
    from concourse.bass_utils import run_bass_kernel_spmd

    f = np.float32
    attr_t = np.zeros((D, EPAD), f)
    attr_t[:, :EDGES] = np.asarray(edge_attr_96).T
    src_pad = np.zeros(EPAD, np.int32)
    src_pad[:EDGES] = np.asarray(src)
    dst_pad = np.full(EPAD, NO_NODE, np.int32)
    dst_pad[:EDGES] = np.asarray(dst)
    first = np.full(GROUPS, 0, np.int32)
    real = -(-EDGES // GE)
    first[:real] = dst_pad[::GE][:real]
    src_blocks = np.ascontiguousarray(
        src_pad.reshape(2 * STEPS, HALF * TPG, LANES).transpose(0, 2, 1))
    dst_cols = np.ascontiguousarray(dst_pad.reshape(GROUPS * TPG, LANES).T)

    w = np.zeros((D + 1, W_COLS), f)
    for at, mat in ((W_EDGE, L0_gnn_W_edge), (W_1, L0_gnn_W1), (W_2, L0_gnn_W2), (W_L, L1_gnn_Wl),
                    (W_R, L1_gnn_Wr)):
        w[:D, at:at + D] = np.asarray(mat).T
    w[D, W_EDGE:W_EDGE + D] = np.asarray(L0_gnn_b_edge)
    w[D, W_2:W_2 + D] = np.asarray(L0_gnn_b2)
    for at, vec in ((C_B1, L0_gnn_b1), (C_BL, L1_gnn_bl), (C_GAMMA, L1_gnn_gamma), (C_BETA, L1_gnn_beta)):
        w[:D, at] = np.asarray(vec)
    w[:, C_EPS] = np.asarray(L0_gnn_eps)

    arrays = {"x": np.ascontiguousarray(x), "edge_attr_t": attr_t, "src_blocks": src_blocks,
              "dst_cols": dst_cols, "dst_first": first.reshape(1, GROUPS), "weights": w,
              "identity": np.eye(LANES, dtype=f)}
    nc = bacc.Bacc("TRN2", target_bir_lowering=False, num_devices=1)
    aps = [nc.dram_tensor(f"in_{n}", a.shape, mybir.dt.from_np(a.dtype), kind="ExternalInput").ap()
           for n, a in arrays.items()]
    out = nc.dram_tensor("out_0", (NODES, D), F32, kind="ExternalOutput").ap()
    graph_layers(nc, *aps, out)
    r = run_bass_kernel_spmd(nc, [{f"in_{n}": a for n, a in arrays.items()}], core_ids=[0])
    return r.results[0]["out_0"]
```

```python
from contextlib import ExitStack

import numpy as np
import concourse.bass as bass
from concourse import mybir

ALU = mybir.AluOpType
ACT = mybir.ActivationFunctionType
AX_X = mybir.AxisListType.X
F32 = mybir.dt.float32
BF16 = mybir.dt.bfloat16
I32 = mybir.dt.int32

NODES, D, EDGES = 6250, 96, 106250
NP, NJ = 125, 2
CN = NP * NJ
CHUNKS = NODES // CN
CW = NJ * D
SPLIT = 120
LANES, TPG = 128, 4
GE = LANES * TPG
SLOTS = 8
HALF = SLOTS // 2
TURNS = -(-EDGES // (GE * SLOTS))
GROUPS = TURNS * SLOTS
EPAD = GROUPS * GE
TESTED = 17
PAIRS = TURNS // 2
LAG = 3
WIN = 64
PPASS2 = 8
GATHER_GROUPS = PPASS2 * 2 * SLOTS
GPU, TPU = 2, 8
UPP = (GROUPS - GATHER_GROUPS) // GPU // PPASS2
UNITS = UPP * PPASS2
DT0 = GATHER_GROUPS * TPG
DTS = UNITS * TPU
DWIN = LANES // TPU
UWIN = 96
NA = -(-NODES // LANES)
NA2 = NA + NA % 2
CHALF = NA2 // 2 * DWIN
PARTS = 7
PA = NA // PARTS
DENSE_STEPS = (UPP + 1) * TPU + 4
DCHUNK = 16
GWIN = 512
GWINS = -(-NODES // GWIN)
SUMS = GWINS * GWIN
LEFT = [*range(2 * PPASS2 - 4, DCHUNK), *range(DCHUNK - 2 + PPASS2, CHUNKS)]
LN_EPS = BN_EPS = 1e-5
NO_NODE = 1 << 20
LOADS = 5
CPL = CHUNKS // LOADS
TPL = CPL * NJ

W_EDGE, W_1, W_2, W_L, W_R = (D * i for i in range(5))
C_B1, C_BL, C_GAMMA, C_BETA, C_EPS = (5 * D + i for i in range(5))
W_COLS = 5 * D + 5

assert (GROUPS - GATHER_GROUPS) == UNITS * GPU and PA * PARTS == NA


def graph_layers(nc, x, edge_attr_t, src_blocks, dst_cols, dst_first, tile_first, column_first, weights,
                 identity, out):
    h_dram = nc.dram_tensor("h_rows", [NODES, D], F32).ap()
    h2_padded = nc.dram_tensor("h2_rows", [NA * LANES, D], F32).ap()
    h2_dram = h2_padded[0:NODES, :]

    with ExitStack() as ctx:
        def sb(name, shape, dt=F32):
            return ctx.enter_context(nc.sbuf_tensor(name, shape, dt))

        def sem(name):
            return ctx.enter_context(nc.semaphore(name))

        x_nm = sb("x_nm", [NP, CHUNKS * CW])
        h_or_pre = sb("h_or_pre", [NP, NODES])
        h_nm = h_or_pre[:, 0:CHUNKS * CW]
        l1_fm = h_or_pre[0:D, :]
        h_or_rdeg = sb("h_or_rdeg", [D, NODES])
        sums0_or_h2 = sb("sums0_or_h2", [LANES, NA * 3 * D // 2])
        sums0 = sums0_or_h2[0:D + 1, 0:SUMS]
        h2_parts = sums0_or_h2[:, :].bitcast(BF16).rearrange("b (a q) -> b a q", q=3 * D)
        sums1 = sb("sums1", [D, SUMS])
        w = sb("w", [D + 1, W_COLS])
        ident = sb("ident", [LANES, LANES])
        ones = sb("ones", [LANES, LANES])
        iota = sb("iota", [LANES, GWIN])
        dst_i = sb("dst_i", [LANES, GROUPS * TPG], I32)
        rel = sb("rel", [LANES, GROUPS * TPG])
        base_i = sb("base_i", [LANES, GROUPS], I32)
        ahead = sb("ahead", [LANES, GROUPS])
        idx = sb("idx", [LANES, 4, HALF * TPG], I32)
        edge_buf = sb("edge_buf", [LANES, NA2 * LANES])
        attr = edge_buf[0:D + 1, 0:HALF * 2 * GE].rearrange("f (q e) -> f q e", q=HALF)
        gsel = edge_buf[:, HALF * 2 * GE:HALF * 2 * GE + TPG * GWIN]
        counts = edge_buf[:, :].bitcast(BF16).rearrange("b (u a n) -> b u a n", u=2, a=NA2)
        gat = sb("gat", [LANES, SLOTS, TPG * D])
        pre = sb("pre", [LANES, 2, TPG * D])
        msg = sb("msg", [LANES, 2, TPG * (D + 1)])
        h2_stage = [t[:, :, :].rearrange("p b n -> p (b n)")[:, 0:PA * D] for t in (pre, msg)]
        sel = sb("sel", [LANES, 2, TPG * WIN])
        slack = sb("slack", [LANES, 16])
        ends = sb("ends", [LANES, 8])
        src_i = sb("src_i", [LANES, DTS], I32)
        src_a16 = sb("src_a16", [LANES, DTS], I32)
        src_b = sb("src_b", [LANES, DTS])
        column = sb("column", [LANES, DTS])
        tile_i = sb("tile_i", [LANES, DTS], I32)
        place_i = sb("place_i", [LANES, UNITS], I32)
        place = sb("place", [LANES, UNITS])
        lane_i = sb("lane_i", [LANES, 1], I32)
        lane = sb("lane", [LANES, 1])
        iota16 = sb("iota16", [LANES, 2 * CHALF], mybir.dt.float16)
        hot_b = sb("hot_b", [LANES, 2, LANES], BF16)
        hot_c = sb("hot_c", [LANES, 2, 2 * CHALF], BF16)
        placer = sb("placer", [LANES, UWIN])
        unit_sum = sb("unit_sum", [LANES, 3, D])
        zeros = sb("zeros", [NA * LANES - NODES, D])
        wide_i = sb("wide_i", [1, 1], I32)
        stats = sb("stats", [NP, TPL, 6])
        moments = sb("moments", [NP, 5, TPL])
        sd = sb("sd", [NP, 2, TPL])
        rstd = sb("rstd", [NP, 2, TPL])
        nmr = sb("nmr", [NP, 2, TPL])
        u = sb("u", [D, CN])
        z = sb("z", [D + 1, CN])
        degrow = sb("degrow", [D + 1, CN])
        h2 = sb("h2", [NP, CW])
        h2t = sb("h2t", [D, CN])
        eps_c = sb("eps_c", [LANES, 1])
        eps1 = sb("eps1", [D + 1, 1])
        bstats = sb("bstats", [D, CHUNKS, 6])
        bmv = sb("bmv", [D, 2])
        bn = sb("bn", [D, 6])

        banks = ctx.enter_context(nc.psum_tensor("banks", [LANES, 8, 512], F32))
        agg_ps = [banks[:, 0, :], banks[:, 1, :]]
        ea_ps = [banks[:, 2, :], banks[:, 3, :]]
        node_ps = [banks[:, b, :] for b in range(4, 8)]
        z_ps, y_ps, t_ps, deg_ps = node_ps
        agg1_ps, l1_ps, placed_ps = banks[:, 0, :], banks[:, 1, 0:CN], banks[:, 1, CN:CN + UWIN]
        unit_ps = [banks[:, 2, :], banks[:, 3, :]]
        count_ps = [banks[:, 4:6, 0:CHALF], banks[:, 6:8, 0:CHALF]]

        def at(start, size):
            return slice(start, start + size) if isinstance(start, int) else bass.ds(start, size)

        def rows_of(rows, c, n=1):
            return rows.rearrange("(c p j) f -> p c (j f)", p=NP, j=NJ)[:, at(c, n), :]

        def chunk_sums(sums, c, rows):
            return sums[rows, at(c * CN, CN)].rearrange("f (p j) -> f j p", j=NJ)

        def tiles(ap):
            return ap.rearrange("f (j p) -> f j p", p=NP)

        rel3 = rel[:, :].rearrange("p (g k) -> p g k", k=TPG)
        sums = [sums0, sums1]
        sum_rows = [D + 1, D]

        x_in = [sem(f"x_in{i}") for i in range(LOADS)]
        w_in, dst_in = sem("w_in"), sem("dst_in")
        consts_set, ones_set = sem("consts_set"), sem("ones_set")
        test_step, bad_summed, wide_ready = sem("test_step"), sem("bad_summed"), sem("wide_ready")
        var_done, sd_done, scale_done = sem("var_done"), sem("sd_done"), sem("scale_done")
        h_done, h_out, h_turned, h_copied = sem("h_done"), sem("h_out"), sem("h_turned"), sem("h_copied")
        mixed, z_mm, z_done, y_mm, x1_done = (sem(n) for n in ("mixed", "z_mm", "z_done", "y_mm", "x1_done"))
        deg_copied, deg_mm, deg_max, rdeg_done = (
            sem(n) for n in ("deg_copied", "deg_mm", "deg_max", "rdeg_done"))
        var2_done, sd2_done, scale2_done = sem("var2_done"), sem("sd2_done"), sem("scale2_done")
        h2_done, h2_turned, h2_copied = sem("h2_done"), sem("h2_turned"), sem("h2_copied")
        h2_out = sem("h2_out")
        r_mm, r_done = sem("r_mm"), sem("r_done")
        mean_done, l1_mm, l1_done, bstat_done = (
            sem(n) for n in ("mean_done", "l1_mm", "l1_done", "bstat_done"))
        bmv_done, bsd_done, affine_done = sem("bmv_done"), sem("bsd_done"), sem("affine_done")
        y1_done, y1_turned, out_done, stored = (
            sem(n) for n in ("y1_done", "y1_turned", "out_done", "stored"))
        dve_step, node_step = sem("dve_step"), sem("node_step")
        wait_carried = sem("wait_carried")
        half_taken = sem("half_taken")

        dense_in, dense_set = sem("dense_in"), sem("dense_set")
        pad_out = sem("pad_out")
        part_in = [sem("part_in0"), sem("part_in1")]
        part_hi, part_rest, part_mid, part_lo = (
            sem(n) for n in ("part_hi", "part_rest", "part_mid", "part_lo"))
        hot_done, counted, count_copied = sem("hot_done"), sem("counted"), sem("count_copied")
        unit_mm, unit_hi, unit_mid, unit_summed = (
            sem(n) for n in ("unit_mm", "unit_hi", "unit_mid", "unit_summed"))
        placer_done, placed, unit_added = sem("placer_done"), sem("placed"), sem("unit_added")

        idx_in = [sem(f"idx_in{b}") for b in range(4)]
        gathered = [sem(f"gathered{s}") for s in range(SLOTS)]
        attr_in = [sem(f"attr_in{q}") for q in range(HALF)]
        ea_done, pre_done, msg_done = sem("ea_done"), sem("pre_done"), sem("msg_done")
        sel_done = [sem(f"sel_done{p}") for p in range(2)]
        agg_done = [sem(f"agg_done{p}") for p in range(2)]
        acc_done = [sem(f"acc_done{p}") for p in range(2)]
        gsel_done = [sem(f"gsel_done{p}") for p in range(2)]
        gagg_done = [sem(f"gagg_done{p}") for p in range(2)]
        gacc_done = [sem(f"gacc_done{p}") for p in range(2)]

        def wait_past(eng, s, i, count):
            if not isinstance(i, int) or count > 0:
                eng.wait_ge(s, count)

        def turns(eng, turn):
            turn(0)
            with eng.Fori(1, TURNS) as i:
                turn(i)

        def whole_chunk(steps, c, n):
            for s in sorted(steps):
                for step in steps[s]:
                    step(c, n)

        def turns_with_nodes(eng, group, steps, flush=None):
            def turn(i, nodes):
                for s in range(SLOTS):
                    group(i, s)
                    for step in steps.get(s, ()) if nodes else ():
                        step(i - LAG, i - LAG)
                if flush:
                    flush(i)
            turn(0, False)
            with eng.Fori(1, LAG) as i:
                turn(i, False)
            with eng.Fori(LAG, TURNS) as i:
                turn(i, True)
            for c in range(TURNS - LAG, CHUNKS):
                whole_chunk(steps, c, c)

        def turns_then_nodes(eng, group, steps, after_edges=None):
            def turn(i):
                for s in range(SLOTS):
                    group(i, s)
            turns(eng, turn)
            if after_edges:
                after_edges()

            whole_chunk(steps, 0, 0)
            with eng.Fori(1, CHUNKS) as c:
                whole_chunk(steps, c, c)

        def pairs_with_dense(eng, group, dense, steps, flush=None):
            def pair(j, nodes):
                for s in range(2 * SLOTS):
                    group(j, s)
                    for n in range(DENSE_STEPS):
                        if n * 2 * SLOTS // DENSE_STEPS == s:
                            dense(j, n)
                    for q, c in enumerate((2 * j - 4, 2 * j - 3, DCHUNK - 2 + j) if nodes else ()):
                        for step in steps.get(s - 5 * q, ()):
                            step(c, 3 * (j - 2) + q)
                if flush:
                    flush(j)
            pair(0, False)
            pair(1, False)
            with eng.Fori(2, PPASS2) as j:
                pair(j, True)
            for n, c in enumerate(LEFT):
                whole_chunk(steps, c, 3 * (PPASS2 - 2) + n)

        def gathers_by(p, i):
            return (p * TURNS + i + 1) * TPG * 16

        block = ctx.enter_context(nc.Block())

        @block.sync
        def _(sp):
            for i in range(LOADS):
                sp.dma_start(x_nm[0:SPLIT, i * CPL * CW:(i + 1) * CPL * CW].rearrange("p (c n) -> p c n", n=CW),
                             rows_of(x, i * CPL, CPL)[0:SPLIT]).then_inc(x_in[i], 16)
            sp.dma_start(w[:, :], weights[:, :]).then_inc(w_in, 16)
            sp.dma_start(dst_i[:, :], dst_cols[:, :]).then_inc(dst_in, 16)
            sp.dma_start(base_i[:, :], dst_first.to_broadcast([LANES, GROUPS])).then_inc(dst_in, 16)
            blocks = slice(DT0 // (HALF * TPG), (DT0 + DTS) // (HALF * TPG))
            sp.dma_start(src_i[:, :].rearrange("p (b k) -> p b k", k=HALF * TPG),
                         src_blocks[blocks].rearrange("b p k -> p b k")).then_inc(dense_in, 16)
            sp.dma_start(tile_i[:, :], tile_first.to_broadcast([LANES, DTS])).then_inc(dense_in, 16)
            sp.dma_start(place_i[:, :], column_first[:, :]).then_inc(dense_in, 16)

            def load_idx(p, j, t, h):
                for s in range(h * HALF, (h + 1) * HALF):
                    wait_past(sp, gathered[s], j, gathers_by(p, 2 * j + t - 2))
                sp.dma_start(idx[:, 2 * t + h, :],
                             src_blocks[at((2 * j + t) * 2 + h, 1)].rearrange("a p k -> (a p) k")
                             ).then_inc(idx_in[2 * t + h], 16)

            def load_turn(j, t, last=False):
                i = 2 * j + t
                for q in range(HALF):
                    if q % 2 == 0:
                        after = (0, j, 1) if t == 0 else (1, 0, 0) if last else (0, j + 1, 0)
                        load_idx(*after, q // 2)
                    wait_past(sp, ea_done, i, (i - 1) * SLOTS + 2 * q + 2)
                    sp.dma_start(attr[0:D, q, :],
                                 edge_attr_t[:, at(i * (SLOTS * GE) + q * 2 * GE, 2 * GE)]
                                 ).then_inc(attr_in[q], 16)

            for h in range(2):
                load_idx(0, 0, 0, h)
            load_turn(0, 0)
            for i in range(LOADS):
                sp.wait_ge(h_done, TPL * (i + 1))
                for a, b in ((0, SPLIT), (SPLIT, NP)):
                    sp.dma_start(rows_of(h_dram, i * CPL, CPL)[a:b],
                                 h_nm[a:b, i * CPL * CW:(i + 1) * CPL * CW].rearrange("p (c n) -> p c n", n=CW)
                                 ).then_inc(h_out, 16)
            load_turn(0, 1)
            with sp.Fori(1, PAIRS - 1) as j:
                for t in range(2):
                    load_turn(j, t)
            for t in range(2):
                load_turn(PAIRS - 1, t, last=True)

            for h in range(2):
                load_idx(1, 0, 1, h)
            def rest_of_indices(pairs):
                with sp.Fori(1, pairs) as j:
                    for t in range(2):
                        for h in range(2):
                            load_idx(1, j, t, h)

            sp.wait_ge(wide_ready, 1)
            wide = sp.value_load(wide_i[0:1, 0:1], min_val=0, max_val=LANES)
            with sp.If(wide < 1):
                sp.wait_ge(pad_out, 16)
                sp.wait_ge(h2_out, 32 * CHUNKS)
                for i in range(PARTS):
                    if i >= 2:
                        sp.wait_ge(part_lo, i - 1)
                    sp.dma_start(h2_stage[i % 2].rearrange("b (a f) -> b a f", f=D),
                                 h2_padded.rearrange("(a b) f -> b a f", b=LANES)[:, i * PA:(i + 1) * PA, :]
                                 ).then_inc(part_in[i % 2], 16)
                rest_of_indices(PPASS2)
            with sp.Else():
                rest_of_indices(PAIRS)

            for i in range(LOADS):
                sp.wait_ge(out_done, CPL * (i + 1))
                for a, b in ((0, SPLIT), (SPLIT, NP)):
                    sp.dma_start(rows_of(out, i * CPL, CPL)[a:b],
                                 x_nm[a:b, i * CPL * CW:(i + 1) * CPL * CW].rearrange("p (c n) -> p c n", n=CW)
                                 ).then_inc(stored, 16)
            sp.wait_ge(stored, 32 * LOADS)

        @block.gpsimd
        def _(pool):
            nc.gpsimd.iota(iota[:, :], pattern=[[1, GWIN]], base=0, channel_multiplier=0,
                           allow_small_or_imprecise_dtypes=True).then_inc(consts_set, 1)
            nc.gpsimd.memset(sums0[:, :], 0.0).then_inc(consts_set, 1)
            nc.gpsimd.memset(sums1[:, :], 0.0).then_inc(consts_set, 1)
            nc.gpsimd.iota(lane_i[:, :], pattern=[[0, 1]], base=0, channel_multiplier=1).then_inc(consts_set, 1)
            nc.gpsimd.iota(iota16[:, :], pattern=[[1, 2 * CHALF]], base=0, channel_multiplier=0,
                           allow_small_or_imprecise_dtypes=True).then_inc(consts_set, 1)
            nc.gpsimd.memset(zeros[:, :], 0.0).then_inc(consts_set, 1)

            def gathers(p, j, table):
                for t in range(2):
                    for h in range(2):
                        pool.wait_ge(idx_in[2 * t + h], 16 * (p * PAIRS + j + 1))
                        wait_past(pool, pre_done if p == 0 else agg_done[1], j,
                                  (2 * j + t - 1) * SLOTS + (h + 1) * HALF)
                        pool.sem_inc(half_taken, 1)
                        for s in range(h * HALF, (h + 1) * HALF):
                            for k in range(TPG):
                                col = (s % HALF) * TPG + k
                                nc.gpsimd.indirect_dma_start(
                                    out=gat[:, s, k * D:(k + 1) * D], out_offset=None, in_=table[:, :],
                                    in_offset=bass.IndirectOffsetOnAxis(
                                        ap=idx[:, 2 * t + h, col:col + 1], axis=0),
                                ).then_inc(gathered[s], 16)

            def pairs(p, table, n):
                gathers(p, 0, table)
                with pool.Fori(1, n) as j:
                    gathers(p, j, table)

            pool.wait_ge(h_out, 32 * LOADS)
            pairs(0, h_dram, PAIRS)
            pool.wait_ge(wide_ready, 1)
            pool.wait_ge(h2_out, 32 * CHUNKS)
            wide = pool.value_load(wide_i[0:1, 0:1], min_val=0, max_val=LANES)
            with pool.If(wide < 1):
                pairs(1, h2_dram, PPASS2)
            with pool.Else():
                pairs(1, h2_dram, PAIRS)

        @block.tensor
        def _(pe):
            pe.wait_ge(w_in, 32)
            for c in range(CHUNKS):
                pe.wait_ge(h_done, NJ * (c + 1))
                if c >= 4:
                    pe.wait_ge(h_copied, c - 3)
                for j in range(NJ):
                    mm = nc.tensor.transpose(node_ps[c % 4][0:D, j * NP:(j + 1) * NP],
                                             h_nm[:, (c * NJ + j) * D:(c * NJ + j + 1) * D],
                                             ident[0:NP, 0:NP])
                mm.then_inc(h_turned, 1)

            pe.wait_ge(ones_set, 3)
            pe.wait_ge(test_step, TESTED)
            nc.tensor.matmul(agg_ps[0][0:1, 0:1], slack[:, 15:16], ones[:, 0:1],
                             start=True, stop=True).then_inc(bad_summed, 1)
            pe.wait_ge(wide_ready, 1)
            wide = pe.value_load(wide_i[0:1, 0:1], min_val=0, max_val=LANES)

            def edge_products(i, s):
                if s % 2 == 0:
                    pe.wait_ge(attr_in[s // 2], 16 * (i + 1))
                wait_past(pe, pre_done, i, i * SLOTS + s - 1)
                for k in range(TPG):
                    a = (s % 2) * GE + k * LANES
                    mm = nc.tensor.matmul(ea_ps[s % 2][:, k * D:(k + 1) * D],
                                          attr[:, s // 2, a:a + LANES],
                                          w[:, W_EDGE:W_EDGE + D], start=True, stop=True)
                mm.then_inc(ea_done, 1)

            def messages(p, s, k):
                if p == 0:
                    return msg[:, s % 2, k * (D + 1):(k + 1) * (D + 1)]
                return gat[:, s, k * D:(k + 1) * D]

            def messages_ready(p, i, s):
                if p == 0:
                    pe.wait_ge(msg_done, i * SLOTS + s + 1)
                else:
                    pe.wait_ge(gathered[s], gathers_by(1, i))

            def sum_group(p, i, s):
                messages_ready(p, i, s)
                pe.wait_ge(sel_done[p], i * SLOTS + s + 1)
                wait_past(pe, acc_done[p], i, i * SLOTS + s - 1)
                for k in range(TPG):
                    mm = nc.tensor.matmul(agg_ps[s % 2][0:sum_rows[p], 0:WIN], messages(p, s, k),
                                          sel[:, s % 2, k * WIN:(k + 1) * WIN],
                                          start=(k == 0), stop=(k == TPG - 1))
                mm.then_inc(agg_done[p], 1)

            def sum_group_general(p, i, s):
                messages_ready(p, i, s)
                for v in range(GWINS):
                    n = (i * SLOTS + s) * GWINS + v
                    pe.wait_ge(gsel_done[p], n + 1)
                    wait_past(pe, gacc_done[p], i, n)
                    for k in range(TPG):
                        mm = nc.tensor.matmul(agg_ps[0][0:sum_rows[p], :], messages(p, s, k),
                                              gsel[:, k * GWIN:(k + 1) * GWIN],
                                              start=(k == 0), stop=(k == TPG - 1))
                    mm.then_inc(gagg_done[p], 1)
                pe.wait_ge(gacc_done[p], (i * SLOTS + s + 1) * GWINS)
                pe.nop().then_inc(agg_done[p], 1)

            def first_product(c, n):
                pe.wait_ge(mixed, n + 1)
                wait_past(pe, z_done, n, n)
                nc.tensor.matmul(z_ps[0:D, 0:CN], w[0:D, W_1:W_1 + D], u[:, :],
                                 start=True, stop=True).then_inc(z_mm, 1)

            def spread_degrees(c, n):
                pe.wait_ge(deg_copied, n + 1)
                wait_past(pe, deg_max, n, n)
                nc.tensor.matmul(deg_ps[0:D, 0:CN], ones[D:D + 1, 0:D], degrow[D:D + 1, :],
                                 start=True, stop=True).then_inc(deg_mm, 1)

            def second_product(c, n):
                pe.wait_ge(z_done, n + 1)
                wait_past(pe, x1_done, n, n)
                for j in range(NJ):
                    mm = nc.tensor.matmul(y_ps[0:NP, j * D:(j + 1) * D], z[:, j * NP:(j + 1) * NP],
                                          w[:, W_2:W_2 + D], start=True, stop=True)
                mm.then_inc(y_mm, 1)

            def turn_h2(c, n):
                pe.wait_ge(h2_done, n + 1)
                wait_past(pe, r_done, n, n)
                for j in range(NJ):
                    mm = nc.tensor.transpose(t_ps[0:D, j * NP:(j + 1) * NP],
                                             h2[:, j * D:(j + 1) * D], ident[0:NP, 0:NP])
                mm.then_inc(h2_turned, 1)

            def root_product(c, n):
                pe.wait_ge(h2_copied, n + 1)
                nc.tensor.matmul(t_ps[0:D, CN:2 * CN], w[0:D, W_R:W_R + D], h2t[:, :],
                                 start=True, stop=True).then_inc(r_mm, 1)

            def mean_product(c, n):
                pe.wait_ge(mean_done, n + 1)
                wait_past(pe, l1_done, n, n)
                nc.tensor.matmul(l1_ps[0:D, :], w[0:D, W_L:W_L + D], u[:, :],
                                 start=True, stop=True).then_inc(l1_mm, 1)

            def gathered_group1(j, s):
                g = j * (2 * SLOTS) + s
                pe.wait_ge(gathered[s % SLOTS], gathers_by(1, 2 * j + s // SLOTS))
                pe.wait_ge(sel_done[1], g + 1)
                wait_past(pe, acc_done[1], j, g)
                for k in range(TPG):
                    mm = nc.tensor.matmul(agg1_ps[0:D, 0:WIN], messages(1, s % SLOTS, k),
                                          sel[:, s % 2, k * WIN:(k + 1) * WIN],
                                          start=(k == 0), stop=(k == TPG - 1))
                mm.then_inc(agg_done[1], 1)

            def dense(j, n):
                if n < UPP * TPU:
                    tile = j * (UPP * TPU) + n
                    pe.wait_ge(hot_done, tile + 1)
                    wait_past(pe, count_copied, j, tile - 1)
                    for q in range(2):
                        mm = nc.tensor.matmul(count_ps[n % 2][:, q, :], hot_b[:, n % 2, :],
                                              hot_c[:, n % 2, q * CHALF:(q + 1) * CHALF],
                                              start=True, stop=True)
                    mm.then_inc(counted, 1)
                if TPU <= n < (UPP + 1) * TPU:
                    u, t = n // TPU - 1, n % TPU
                    unit = j * UPP + u
                    if t == 0:
                        pe.wait_ge(count_copied, (unit + 1) * TPU)
                        if u >= 2:
                            pe.wait_ge(unit_summed, unit - 1)
                        else:
                            wait_past(pe, unit_summed, j, j * UPP)
                        if isinstance(j, int) and j == 0 and u == 0:
                            pe.wait_ge(part_lo, PARTS)
                    for a in range(NA * t // TPU, NA * (t + 1) // TPU):
                        mm = nc.tensor.matmul(unit_ps[u % 2][:, 0:3 * D], counts[:, u % 2, a, :],
                                              h2_parts[:, a, :], start=(a == 0), stop=(a == NA - 1))
                    if t == TPU - 1:
                        mm.then_inc(unit_mm, 1)
                if n >= 2 * TPU and n % TPU == 3:
                    unit = j * UPP + n // TPU - 2
                    pe.wait_ge(unit_summed, unit + 1)
                    pe.wait_ge(placer_done, unit + 1)
                    wait_past(pe, unit_added, j, unit)
                    nc.tensor.matmul(placed_ps[0:D, :], unit_sum[:, 2, :], placer[:, :],
                                     start=True, stop=True).then_inc(placed, 1)

            steps0 = {1: [first_product, spread_degrees], 2: [second_product], 5: [turn_h2],
                      6: [root_product]}
            steps1 = {1: [mean_product]}

            def group0(i, s):
                edge_products(i, s)
                if s > 0:
                    sum_group(0, i, s - 1)

            def group0_general(i, s):
                edge_products(i, s)
                sum_group_general(0, i, s)

            with pe.If(wide < 1):
                turns_with_nodes(pe, group0, steps0, lambda i: sum_group(0, i, SLOTS - 1))
            with pe.Else():
                turns_then_nodes(pe, group0_general, steps0)
            with pe.If(wide < 1):
                pairs_with_dense(pe, gathered_group1, dense, steps1)
            with pe.Else():
                turns_then_nodes(pe, lambda i, s: sum_group_general(1, i, s), steps1)

            for c in range(CHUNKS):
                pe.wait_ge(y1_done, c + 1)
                if c >= 4:
                    pe.wait_ge(out_done, c - 3)
                for j in range(NJ):
                    a = c * CN + j * NP
                    mm = nc.tensor.transpose(node_ps[c % 4][0:NP, j * D:(j + 1) * D],
                                             l1_fm[:, a:a + NP], ident[0:D, 0:D])
                mm.then_inc(y1_turned, 1)

        @block.scalar
        def _(act):
            for i in range(LOADS):
                act.dma_start(x_nm[SPLIT:NP, i * CPL * CW:(i + 1) * CPL * CW].rearrange("p (c n) -> p c n", n=CW),
                              rows_of(x, i * CPL, CPL)[SPLIT:NP]).then_inc(x_in[i], 16)
            act.dma_start(ident[:, :], identity[:, :]).then_inc(w_in, 16)

            act.wait_ge(ones_set, 1)
            for i in range(LOADS):
                act.wait_ge(var_done, i + 1)
                if i >= 2:
                    act.wait_ge(scale_done, i - 1)
                nc.scalar.activation(sd[:, i % 2, :], moments[:, 4, :], ACT.Sqrt, scale=1.0 / D,
                                     bias=eps_c[0:NP, :]).then_inc(sd_done, 1)
                act.wait_ge(scale_done, i + 1)
                for t in range(TPL):
                    a = (i * TPL + t) * D
                    nc.scalar.activation(h_nm[:, a:a + D], x_nm[:, a:a + D], ACT.Relu,
                                         bias=nmr[:, i % 2, t:t + 1], scale=rstd[:, i % 2, t:t + 1]
                                         ).then_inc(h_done, 1)

            act.wait_ge(ones_set, 5)
            act.wait_ge(wide_ready, 1)
            wide = act.value_load(wide_i[0:1, 0:1], min_val=0, max_val=LANES)

            def relu_messages(i, s):
                act.wait_ge(pre_done, i * SLOTS + s + 1)
                wait_past(act, agg_done[0], i, i * SLOTS + s - 1)
                nc.scalar.activation(
                    msg[:, s % 2, :].rearrange("p (k f) -> p k f", f=D + 1)[:, :, 0:D],
                    pre[:, s % 2, :].rearrange("p (k f) -> p k f", f=D), ACT.Relu).then_inc(msg_done, 1)

            def relu_z(c, n):
                act.wait_ge(z_mm, n + 1)
                wait_past(act, y_mm, n, n)
                nc.scalar.activation(z[0:D, :], z_ps[0:D, 0:CN], ACT.Relu,
                                     bias=w[0:D, C_B1:C_B1 + 1]).then_inc(z_done, 1)

            def copy_degrees(c, n):
                act.wait_ge(mixed, n + 1)
                wait_past(act, deg_mm, n, n)
                nc.scalar.activation(tiles(degrow[D:D + 1, :]), chunk_sums(sums0, c, slice(D, D + 1)),
                                     ACT.Identity).then_inc(deg_copied, 1)

            def sd_h2(c, n):
                act.wait_ge(var2_done, n + 1)
                nc.scalar.activation(sd[:, 0, 0:NJ], moments[:, 4, 0:NJ], ACT.Sqrt, scale=1.0 / D,
                                     bias=eps_c[0:NP, :]).then_inc(sd2_done, 1)

            def relu_h2(c, n):
                act.wait_ge(scale2_done, n + 1)
                wait_past(act, h2_turned, n, n)
                wait_past(act, h2_out, c, 32 * c)
                for j in range(NJ):
                    ins = nc.scalar.activation(h2[:, j * D:(j + 1) * D], x_nm[:, at(c * CW + j * D, D)],
                                               ACT.Relu, bias=nmr[:, 0, j:j + 1], scale=rstd[:, 0, j:j + 1])
                ins.then_inc(h2_done, 1)
                act.wait_ge(h2_done, n + 1)
                for a, b in ((0, SPLIT), (SPLIT, NP)):
                    act.dma_start(rows_of(h2_dram, c)[a:b].rearrange("p c n -> p (c n)"),
                                  h2[a:b, :]).then_inc(h2_out, 16)

            def copy_h2(c, n):
                act.wait_ge(h2_turned, n + 1)
                wait_past(act, r_mm, n, n)
                nc.scalar.activation(h2t[:, :], t_ps[0:D, 0:CN], ACT.Identity).then_inc(h2_copied, 1)

            def root_bias(c, n):
                act.wait_ge(r_mm, n + 1)
                nc.scalar.activation(l1_fm[:, at(c * CN, CN)], t_ps[0:D, CN:2 * CN], ACT.Identity,
                                     bias=w[0:D, C_BL:C_BL + 1]).then_inc(r_done, 1)

            act.wait_ge(h_out, 32 * LOADS)
            act.wait_ge(h_turned, CHUNKS)
            act.wait_ge(consts_set, 6)
            act.dma_start(h2_padded[NODES:NA * LANES, :], zeros[:, :]).then_inc(pad_out, 16)
            steps0 = {0: [copy_degrees], 1: [relu_z], 3: [sd_h2], 4: [relu_h2], 5: [copy_h2], 6: [root_bias]}
            with act.If(wide < 1):
                turns_with_nodes(act, relu_messages, steps0)
            with act.Else():
                turns_then_nodes(act, relu_messages, steps0)

            def copy_counts(j, n):
                if n < UPP * TPU:
                    tile, u, t = j * (UPP * TPU) + n, n // TPU, n % TPU
                    act.wait_ge(counted, tile + 1)
                    if t == 0:
                        if u >= 2:
                            act.wait_ge(unit_mm, j * UPP + u - 1)
                        else:
                            wait_past(act, unit_mm, j, j * UPP)
                    nc.scalar.activation(
                        counts[:, u % 2, :, t * DWIN:(t + 1) * DWIN].rearrange("b (q a) d -> b q a d", q=2),
                        count_ps[n % 2].rearrange("b q (a d) -> b q a d", d=DWIN),
                        ACT.Identity).then_inc(count_copied, 1)
                if n >= 2 * TPU and n % TPU == 0:
                    unit = j * UPP + n // TPU - 2
                    act.wait_ge(unit_mm, unit + 1)
                    wait_past(act, unit_summed, j, unit)
                    nc.scalar.activation(unit_sum[:, 0, :], unit_ps[(n // TPU) % 2][:, 0:D],
                                         ACT.Identity).then_inc(unit_hi, 1)

            with act.If(wide < 1):
                for i in range(PARTS):
                    part = h2_parts[:, i * PA:(i + 1) * PA, :]
                    stage = h2_stage[i % 2].rearrange("b (a f) -> b a f", f=D)
                    act.wait_ge(part_in[i % 2], 16 * (i // 2 + 1))
                    nc.scalar.activation(part[:, :, 0:D], stage, ACT.Identity).then_inc(part_hi, 1)
                    act.wait_ge(part_rest, i + 1)
                    nc.scalar.activation(part[:, :, D:2 * D], stage, ACT.Identity).then_inc(part_mid, 1)
                pairs_with_dense(act, lambda j, s: None, copy_counts, {})

            act.wait_ge(bmv_done, 1)
            nc.scalar.activation(bn[:, 0:1], bmv[:, 1:2], ACT.Sqrt, bias=eps_c[0:D, :]).then_inc(bsd_done, 1)
            act.wait_ge(affine_done, 1)
            for c in range(CHUNKS):
                part = l1_fm[:, c * CN:(c + 1) * CN]
                nc.scalar.activation(part, part, ACT.Relu, bias=bn[:, 4:5], scale=bn[:, 2:3]
                                     ).then_inc(y1_done, 1)

        @block.vector
        def _(dve):
            nc.vector.memset(eps_c[:, :], LN_EPS).then_inc(ones_set, 1)
            nc.vector.memset(ones[:, :], 1.0).then_inc(ones_set, 1)
            nc.vector.memset(attr[D:D + 1, :, :], 1.0).then_inc(ones_set, 1)
            nc.vector.memset(z[D:D + 1, :], 1.0).then_inc(ones_set, 1)
            nc.vector.memset(msg[:, :, :], 1.0).then_inc(ones_set, 1)

            dve_steps = [0]

            def in_order(ins):
                dve_steps[0] += 1
                ins.then_inc(dve_step, 1)
                dve.wait_ge(dve_step, dve_steps[0])

            def sums_of_means(n):
                mean_e, m2_e, mean_o, m2_o = (stats[:, 0:n, f] for f in (1, 2, 4, 5))
                nc.vector.tensor_tensor(moments[:, 0, 0:n], mean_e, mean_o, ALU.add)
                nc.vector.tensor_tensor(moments[:, 2, 0:n], m2_e, m2_o, ALU.add)
                return nc.vector.tensor_tensor(moments[:, 1, 0:n], mean_e, mean_o, ALU.subtract)

            def squared_difference(n):
                return nc.vector.tensor_tensor(moments[:, 3, 0:n], moments[:, 1, 0:n], moments[:, 1, 0:n],
                                               ALU.mult)

            def d_times_variance(n):
                return nc.vector.scalar_tensor_tensor(
                    out=moments[:, 4, 0:n], in0=moments[:, 3, 0:n], scalar=D / 4.0,
                    in1=moments[:, 2, 0:n], op0=ALU.mult, op1=ALU.add)

            def minus_mean_rstd(b, n):
                return nc.vector.scalar_tensor_tensor(
                    out=nmr[:, b, 0:n], in0=moments[:, 0, 0:n], scalar=-0.5, in1=rstd[:, b, 0:n],
                    op0=ALU.mult, op1=ALU.mult)

            for i in range(LOADS):
                dve.wait_ge(x_in[i], 32)
                for t in range(TPL):
                    a = (i * TPL + t) * D
                    ins = nc.vector.bn_stats(stats[:, t, :], x_nm[:, a:a + D])
                in_order(ins)
                in_order(sums_of_means(TPL))
                in_order(squared_difference(TPL))
                d_times_variance(TPL).then_inc(var_done, 1)
                dve.wait_ge(sd_done, i + 1)
                if i >= 2:
                    dve.wait_ge(h_done, TPL * (i - 1))
                in_order(nc.vector.reciprocal(rstd[:, i % 2, :], sd[:, i % 2, :]))
                minus_mean_rstd(i % 2, TPL).then_inc(scale_done, 1)

            def tested(ins):
                ins.then_inc(test_step, 1)
                tests[0] += 1
                dve.wait_ge(test_step, tests[0])

            tests = [0]
            dve.wait_ge(dst_in, 32)
            dve.wait_ge(dense_in, 48)
            dve.wait_ge(consts_set, 6)
            dst_dense = dst_i[:, DT0:DT0 + DTS]
            nc.vector.tensor_scalar(src_a16[:, :], src_i[:, :], 7, 4, ALU.logical_shift_right,
                                    ALU.logical_shift_left)
            tested(nc.vector.tensor_tensor(column[:, :], dst_dense, tile_i[:, :], ALU.subtract))
            full, part = EDGES // LANES, EDGES % LANES
            lo, hi = slack[:, 4:5], slack[:, 12:13]
            nc.vector.tensor_reduce(lo, column[:, 0:full - DT0], AX_X, ALU.min)
            tested(nc.vector.tensor_reduce(hi, column[:, 0:full - DT0], AX_X, ALU.max))
            last = column[0:part, full - DT0:full - DT0 + 1]
            nc.vector.tensor_tensor(slack[0:part, 4:5], slack[0:part, 4:5], last, ALU.min)
            tested(nc.vector.tensor_tensor(slack[0:part, 12:13], slack[0:part, 12:13], last, ALU.max))
            nc.vector.tensor_scalar(slack[:, 5:6], hi, -1.0, float(DWIN - 1), ALU.mult, ALU.add)
            nc.vector.tensor_scalar(src_i[:, :], src_i[:, :], LANES - 1, None, ALU.bitwise_and)
            nc.vector.tensor_scalar(lane_i[:, :], lane_i[:, :], DWIN - 1, None, ALU.bitwise_and)
            tested(nc.vector.tensor_tensor(column[:, :], column[:, :], src_a16[:, :], ALU.add))
            nc.vector.tensor_copy(src_b[:, :], src_i[:, :])
            nc.vector.tensor_copy(lane[:, :], lane_i[:, :])
            tested(nc.vector.tensor_tensor(place[:, :], place_i[:, :], base_i[:, GATHER_GROUPS::GPU],
                                           ALU.subtract))
            nc.vector.tensor_reduce(slack[:, 6:7], place[:, :], AX_X, ALU.min)
            tested(nc.vector.tensor_reduce(slack[:, 13:14], place[:, :], AX_X, ALU.max))
            nc.vector.tensor_scalar(slack[:, 7:8], slack[:, 13:14], -1.0, float(UWIN - DWIN), ALU.mult, ALU.add)
            tested(nc.vector.tensor_scalar(place[:, :], place[:, :], lane[:, 0:1], None, ALU.add))

            tested(nc.vector.tensor_tensor(rel3, dst_i[:, :].rearrange("p (g k) -> p g k", k=TPG),
                                           base_i[:, :].unsqueeze(2).to_broadcast([LANES, GROUPS, TPG]),
                                           ALU.subtract))
            tested(nc.vector.tensor_tensor(ahead[:, 1:GROUPS], base_i[:, 1:GROUPS], base_i[:, 0:GROUPS - 1],
                                           ALU.subtract))
            nc.vector.tensor_reduce(slack[:, 0:1], rel[:, 0:full], AX_X, ALU.min)
            nc.vector.tensor_reduce(slack[:, 14:15], rel[:, 0:full], AX_X, ALU.max)
            tested(nc.vector.tensor_reduce(slack[:, 2:3], ahead[:, 1:GROUPS], AX_X, ALU.min))
            nc.vector.tensor_tensor(slack[0:part, 0:1], slack[0:part, 0:1], rel[0:part, full:full + 1], ALU.min)
            nc.vector.tensor_tensor(slack[0:part, 14:15], slack[0:part, 14:15], rel[0:part, full:full + 1],
                                    ALU.max)
            taken = TURNS - LAG
            tested(nc.vector.scalar_tensor_tensor(
                out=ahead[:, 0:taken], in0=iota[:, 0:taken], scalar=-float(CN),
                in1=base_i[:, LAG * SLOTS::SLOTS], op0=ALU.mult, op1=ALU.add))
            nc.vector.tensor_scalar(slack[:, 1:2], slack[:, 14:15], -1.0, float(WIN - 1), ALU.mult, ALU.add)
            tested(nc.vector.tensor_reduce(ends[:, 0:1], ahead[:, 0:taken], AX_X, ALU.min))
            nc.vector.tensor_scalar(slack[:, 3:4], ends[:, 0:1], -float(CN), None, ALU.add)
            nc.vector.tensor_scalar(slack[:, 8:9], base_i[:, GATHER_GROUPS - 1:GATHER_GROUPS], -1.0,
                                    float(DCHUNK * CN - WIN), ALU.mult, ALU.add)
            per_pair = UPP * GPU
            starts = base_i[:, GATHER_GROUPS + 2 * per_pair::per_pair]
            tested(nc.vector.scalar_tensor_tensor(
                out=ahead[:, 0:PPASS2 - 2], in0=iota[:, 0:PPASS2 - 2], scalar=-float(CN), in1=starts,
                op0=ALU.mult, op1=ALU.add))
            tested(nc.vector.tensor_reduce(ends[:, 1:2], ahead[:, 0:PPASS2 - 2], AX_X, ALU.min))
            tested(nc.vector.tensor_scalar(slack[:, 9:10], ends[:, 1:2], -float((DCHUNK + 1) * CN), None,
                                           ALU.add))
            tested(nc.vector.tensor_reduce(slack[:, 10:11], slack[:, 0:10], AX_X, ALU.min))
            nc.vector.tensor_scalar(slack[:, 15:16], slack[:, 10:11], 0.0, None, ALU.is_lt).then_inc(test_step, 1)
            assert tests[0] + 1 == TESTED

            for c in range(CHUNKS):
                dve.wait_ge(h_turned, c + 1)
                nc.vector.tensor_copy(h_or_rdeg[:, c * CN:(c + 1) * CN], node_ps[c % 4][0:D, 0:CN]
                                      ).then_inc(h_copied, 1)
            dve.wait_ge(bad_summed, 1)
            nc.vector.tensor_copy(wide_i[0:1, 0:1], agg_ps[0][0:1, 0:1]).then_inc(wide_ready, 1)
            dve.wait_ge(wide_ready, 1)
            wide = dve.value_load(wide_i[0:1, 0:1], min_val=0, max_val=LANES)
            dve.wait_ge(w_in, 32)
            in_order(nc.vector.tensor_scalar(eps1[:, :], w[:, C_EPS:C_EPS + 1], 1.0, None, ALU.add))
            dve.wait_ge(h_copied, CHUNKS)

            def add_gathered(i, s):
                dve.wait_ge(ea_done, i * SLOTS + s + 1)
                dve.wait_ge(gathered[s], gathers_by(0, i))
                wait_past(dve, msg_done, i, i * SLOTS + s - 1)
                nc.vector.tensor_tensor(pre[:, s % 2, :], ea_ps[s % 2][:, 0:TPG * D], gat[:, s, :],
                                        ALU.add).then_inc(pre_done, 1)

            def select(p, i, s):
                wait_past(dve, agg_done[p], i, i * SLOTS + s - 1)
                r = rel[:, at((i * SLOTS + s) * TPG, TPG)]
                nc.vector.tensor_tensor(
                    sel[:, s % 2, :].rearrange("p (k n) -> p k n", n=WIN),
                    iota[:, 0:WIN].unsqueeze(1).to_broadcast([LANES, TPG, WIN]),
                    r.unsqueeze(2).to_broadcast([LANES, TPG, WIN]),
                    ALU.is_equal).then_inc(sel_done[p], 1)

            def add_group(p, i, s):
                g = i * SLOTS + s
                dve.wait_ge(agg_done[p], g + 1)
                start = dve.value_load(base_i[0:1, at(g, 1)], min_val=0, max_val=NODES - 1)
                window = sums[p][0:sum_rows[p], bass.ds(start, WIN)]
                wait_past(dve, acc_done[p], i, g)
                nc.vector.tensor_tensor(window, window, agg_ps[s % 2][0:sum_rows[p], 0:WIN],
                                        ALU.add).then_inc(acc_done[p], 1)

            def group(p):
                def of_slot(i, s):
                    select(p, i, s)
                    if p == 0:
                        add_gathered(i, s)
                    if s > 0:
                        add_group(p, i, s - 1)
                return of_slot

            def group_general(p):
                def of_slot(i, s):
                    if p == 0:
                        add_gathered(i, s)
                    g = i * SLOTS + s
                    first = isinstance(i, int) and g == 0
                    d = dst_i[:, at(g * TPG, TPG)]
                    for v in range(GWINS):
                        n = g * GWINS + v
                        if v > 0 or not first:
                            dve.wait_ge(gagg_done[p], n)
                        nc.vector.scalar_tensor_tensor(
                            out=gsel[:, :].rearrange("p (k n) -> p k n", n=GWIN),
                            in0=iota[:, :].unsqueeze(1).to_broadcast([LANES, TPG, GWIN]),
                            scalar=float(v * GWIN),
                            in1=d.unsqueeze(2).to_broadcast([LANES, TPG, GWIN]),
                            op0=ALU.add, op1=ALU.is_equal).then_inc(gsel_done[p], 1)
                        dve.wait_ge(gagg_done[p], n + 1)
                        if v > 0 or not first:
                            dve.wait_ge(gacc_done[p], n)
                        part = sums[p][0:sum_rows[p], v * GWIN:(v + 1) * GWIN]
                        nc.vector.tensor_tensor(part, part, agg_ps[0][0:sum_rows[p], :],
                                                ALU.add).then_inc(gacc_done[p], 1)
                return of_slot

            def mix(c, n):
                wait_past(dve, z_mm, n, n)
                nc.vector.scalar_tensor_tensor(
                    out=tiles(u[:, :]), in0=tiles(h_or_rdeg[:, at(c * CN, CN)]), scalar=eps1[0:D, :],
                    in1=chunk_sums(sums0, c, slice(0, D)), op0=ALU.mult, op1=ALU.add).then_inc(mixed, 1)

            def clamp_degrees(c, n):
                dve.wait_ge(deg_mm, n + 1)
                dve.wait_ge(mixed, n + 1)
                nc.vector.tensor_scalar(h_or_rdeg[:, at(c * CN, CN)], deg_ps[0:D, 0:CN], 1.0, None,
                                        ALU.max).then_inc(deg_max, 1)

            def invert_degrees(c, n):
                dve.wait_ge(deg_max, n + 1)
                carry_wait()
                part = h_or_rdeg[:, at(c * CN, CN)]
                nc.vector.reciprocal(part, part).then_inc(rdeg_done, 1)

            def residual(c, n):
                dve.wait_ge(y_mm, n + 1)
                part = x_nm[:, at(c * CW, CW)]
                nc.vector.tensor_tensor(part, part, y_ps[0:NP, 0:CW], ALU.add).then_inc(x1_done, 1)

            def carry_wait():
                dve.sem_inc(wait_carried, 1)

            NODE_STEPS = 4

            def h2_stats(c, n):
                dve.wait_ge(x1_done, n + 1)
                wait_past(dve, h2_done, n, n)
                carry_wait()
                for j in range(NJ):
                    ins = nc.vector.bn_stats(stats[:, j, :], x_nm[:, at(c * CW + j * D, D)])
                ins.then_inc(node_step, 1)
                dve.wait_ge(node_step, n * NODE_STEPS + 1)
                sums_of_means(NJ).then_inc(node_step, 1)
                dve.wait_ge(node_step, n * NODE_STEPS + 2)
                squared_difference(NJ).then_inc(node_step, 1)
                dve.wait_ge(node_step, n * NODE_STEPS + 3)
                d_times_variance(NJ).then_inc(var2_done, 1)

            def h2_scales(c, n):
                dve.wait_ge(sd2_done, n + 1)
                nc.vector.reciprocal(rstd[:, 0, 0:NJ], sd[:, 0, 0:NJ]).then_inc(node_step, 1)
                dve.wait_ge(node_step, n * NODE_STEPS + 4)
                minus_mean_rstd(0, NJ).then_inc(scale2_done, 1)

            def mean(c, n):
                wait_past(dve, l1_mm, n, n)
                nc.vector.tensor_tensor(tiles(u[:, :]), chunk_sums(sums1, c, slice(0, D)),
                                        tiles(h_or_rdeg[:, at(c * CN, CN)]), ALU.mult).then_inc(mean_done, 1)

            def add_root(c, n):
                dve.wait_ge(l1_mm, n + 1)
                part = l1_fm[:, at(c * CN, CN)]
                nc.vector.tensor_tensor(part, part, l1_ps[0:D, :], ALU.add).then_inc(l1_done, 1)

            def batch_stats(c, n):
                dve.wait_ge(l1_done, n + 1)
                carry_wait()
                nc.vector.bn_stats(bstats[:, at(c, 1), :].rearrange("f c s -> f (c s)"),
                                   l1_fm[:, at(c * CN, CN)]).then_inc(bstat_done, 1)

            def group1(j, s):
                g = j * (2 * SLOTS) + s
                wait_past(dve, agg_done[1], j, g - 1)
                nc.vector.tensor_tensor(
                    sel[:, s % 2, :].rearrange("p (k n) -> p k n", n=WIN),
                    iota[:, 0:WIN].unsqueeze(1).to_broadcast([LANES, TPG, WIN]),
                    rel[:, at(g * TPG, TPG)].unsqueeze(2).to_broadcast([LANES, TPG, WIN]),
                    ALU.is_equal).then_inc(sel_done[1], 1)
                if s > 0:
                    add_group1(j, s - 1, -(-DENSE_STEPS * s // (2 * SLOTS)))

            def units_added(j, n):
                return j * UPP + min(max(n - TPU - 4, 0) // TPU, UPP)

            def add_group1(j, s, n):
                g = j * (2 * SLOTS) + s
                dve.wait_ge(agg_done[1], g + 1)
                start = dve.value_load(base_i[0:1, at(g, 1)], min_val=0, max_val=NODES - 1)
                window = sums1[:, bass.ds(start, WIN)]
                wait_past(dve, acc_done[1], j, g)
                wait_past(dve, unit_added, j, units_added(j, n))
                nc.vector.tensor_tensor(window, window, agg1_ps[0:D, 0:WIN], ALU.add).then_inc(acc_done[1], 1)

            def hot(j, n):
                tile = j * (UPP * TPU) + n
                wait_past(dve, counted, j, tile - 1)
                nc.vector.tensor_scalar(hot_b[:, n % 2, :], iota16[:, 0:LANES], src_b[:, at(tile, 1)], None,
                                        ALU.is_equal)
                nc.vector.tensor_scalar(hot_c[:, n % 2, :], iota16[:, :], column[:, at(tile, 1)], None,
                                        ALU.is_equal).then_inc(hot_done, 1)

            def dense(j, n):
                if n == 0:
                    hot(j, 0)
                if n + 1 < UPP * TPU:
                    hot(j, n + 1)
                if n >= 2 * TPU and n % TPU == 1:
                    unit = j * UPP + n // TPU - 2
                    ps = unit_ps[(n // TPU) % 2]
                    wait_past(dve, placed, j, unit)
                    nc.vector.tensor_scalar(placer[:, :], iota[:, 0:UWIN], place[:, at(unit, 1)], None,
                                            ALU.is_equal).then_inc(placer_done, 1)
                    dve.wait_ge(unit_hi, unit + 1)
                    nc.vector.tensor_tensor(unit_sum[:, 1, :], ps[:, D:2 * D], unit_sum[:, 0, :],
                                            ALU.add).then_inc(unit_mid, 1)
                    dve.wait_ge(unit_mid, unit + 1)
                    nc.vector.tensor_tensor(unit_sum[:, 2, :], ps[:, 2 * D:3 * D], unit_sum[:, 1, :],
                                            ALU.add).then_inc(unit_summed, 1)
                if n >= 2 * TPU and n % TPU == 3:
                    unit = j * UPP + n // TPU - 2
                    dve.wait_ge(placed, unit + 1)
                    g = GATHER_GROUPS + unit * GPU
                    start = dve.value_load(base_i[0:1, at(g, 1)], min_val=0, max_val=NODES - 1)
                    window = sums1[:, bass.ds(start, UWIN)]
                    wait_past(dve, unit_added, j, unit)
                    wait_past(dve, acc_done[1], j, j * (2 * SLOTS) + n * 2 * SLOTS // DENSE_STEPS)
                    nc.vector.tensor_tensor(window, window, placed_ps[0:D, :], ALU.add
                                            ).then_inc(unit_added, 1)

            def flush1(j):
                add_group1(j, 2 * SLOTS - 1, DENSE_STEPS)
                dve.wait_ge(acc_done[1], (j + 1) * (2 * SLOTS))
                dve.wait_ge(unit_added, (j + 1) * UPP)

            steps0 = {0: [mix], 1: [clamp_degrees, invert_degrees], 2: [residual, h2_stats], 3: [h2_scales]}
            steps1 = {0: [mean], 2: [add_root, batch_stats]}

            def flush(p):
                def of_turn(i):
                    add_group(p, i, SLOTS - 1)
                    dve.wait_ge(acc_done[p], (i + 1) * SLOTS)
                return of_turn

            def all_added(p):
                return lambda: dve.wait_ge(gacc_done[p], GROUPS * GWINS)

            with dve.If(wide < 1):
                turns_with_nodes(dve, group(0), steps0, flush(0))
            with dve.Else():
                turns_then_nodes(dve, group_general(0), steps0, all_added(0))
            dve.wait_ge(r_done, CHUNKS)
            dve.wait_ge(rdeg_done, CHUNKS)
            with dve.If(wide < 1):
                for i in range(PARTS):
                    part = h2_parts[:, i * PA:(i + 1) * PA, :]
                    stage = h2_stage[i % 2].rearrange("b (a f) -> b a f", f=D)
                    dve.wait_ge(part_hi, i + 1)
                    nc.vector.tensor_tensor(stage, stage, part[:, :, 0:D], ALU.subtract).then_inc(part_rest, 1)
                    dve.wait_ge(part_mid, i + 1)
                    nc.vector.tensor_tensor(part[:, :, 2 * D:3 * D], stage, part[:, :, D:2 * D],
                                            ALU.subtract).then_inc(part_lo, 1)
                pairs_with_dense(dve, group1, dense, steps1, flush1)
            with dve.Else():
                turns_then_nodes(dve, group_general(1), steps1, all_added(1))

            dve.wait_ge(bstat_done, CHUNKS)
            nc.vector.bn_aggr(bmv[:, :], bstats[:, :, :].rearrange("f c s -> f (c s)")).then_inc(bmv_done, 1)
            dve.wait_ge(bsd_done, 1)
            in_order(nc.vector.reciprocal(bn[:, 1:2], bn[:, 0:1]))
            in_order(nc.vector.tensor_tensor(bn[:, 2:3], bn[:, 1:2], w[0:D, C_GAMMA:C_GAMMA + 1], ALU.mult))
            in_order(nc.vector.tensor_tensor(bn[:, 3:4], bn[:, 2:3], bmv[:, 0:1], ALU.mult))
            nc.vector.tensor_tensor(bn[:, 4:5], w[0:D, C_BETA:C_BETA + 1], bn[:, 3:4],
                                    ALU.subtract).then_inc(affine_done, 1)
            for c in range(CHUNKS):
                dve.wait_ge(y1_turned, c + 1)
                part = x_nm[:, c * CW:(c + 1) * CW]
                nc.vector.tensor_tensor(part, part, node_ps[c % 4][0:NP, 0:CW], ALU.add).then_inc(out_done, 1)


def kernel(x, src, dst, edge_attr_96, L0_gnn_W_edge, L0_gnn_b_edge, L0_gnn_eps, L0_gnn_W1, L0_gnn_b1,
           L0_gnn_W2, L0_gnn_b2, L1_gnn_Wl, L1_gnn_bl, L1_gnn_Wr, L1_gnn_gamma, L1_gnn_beta):
    import concourse.bacc as bacc
    from concourse.bass_utils import run_bass_kernel_spmd

    f = np.float32
    attr_t = np.zeros((D, EPAD), f)
    attr_t[:, :EDGES] = np.asarray(edge_attr_96).T
    src_pad = np.zeros(EPAD, np.int32)
    src_pad[:EDGES] = np.asarray(src)
    dst_pad = np.full(EPAD, NO_NODE, np.int32)
    dst_pad[:EDGES] = np.asarray(dst)
    first = np.full(GROUPS, 0, np.int32)
    real = -(-EDGES // GE)
    first[:real] = dst_pad[::GE][:real]
    tile_first = dst_pad[np.minimum(np.arange(DT0, DT0 + DTS) * LANES, EDGES - 1)]
    column_first = np.ascontiguousarray(np.repeat(tile_first.reshape(UNITS, TPU).T, DWIN, axis=0))
    src_blocks = np.ascontiguousarray(
        src_pad.reshape(2 * TURNS, HALF * TPG, LANES).transpose(0, 2, 1))
    dst_cols = np.ascontiguousarray(dst_pad.reshape(GROUPS * TPG, LANES).T)

    w = np.zeros((D + 1, W_COLS), f)
    for at, mat in ((W_EDGE, L0_gnn_W_edge), (W_1, L0_gnn_W1), (W_2, L0_gnn_W2), (W_L, L1_gnn_Wl),
                    (W_R, L1_gnn_Wr)):
        w[:D, at:at + D] = np.asarray(mat).T
    w[D, W_EDGE:W_EDGE + D] = np.asarray(L0_gnn_b_edge)
    w[D, W_2:W_2 + D] = np.asarray(L0_gnn_b2)
    for at, vec in ((C_B1, L0_gnn_b1), (C_BL, L1_gnn_bl), (C_GAMMA, L1_gnn_gamma), (C_BETA, L1_gnn_beta)):
        w[:D, at] = np.asarray(vec)
    w[:, C_EPS] = np.asarray(L0_gnn_eps)

    arrays = {"x": np.ascontiguousarray(x), "edge_attr_t": attr_t, "src_blocks": src_blocks,
              "dst_cols": dst_cols, "dst_first": first.reshape(1, GROUPS),
              "tile_first": tile_first.reshape(1, DTS), "column_first": column_first, "weights": w,
              "identity": np.eye(LANES, dtype=f)}
    nc = bacc.Bacc("TRN2", target_bir_lowering=False, num_devices=1)
    aps = [nc.dram_tensor(f"in_{n}", a.shape, mybir.dt.from_np(a.dtype), kind="ExternalInput").ap()
           for n, a in arrays.items()]
    out = nc.dram_tensor("out_0", (NODES, D), F32, kind="ExternalOutput").ap()
    graph_layers(nc, *aps, out)
    r = run_bass_kernel_spmd(nc, [{f"in_{n}": a for n, a in arrays.items()}], core_ids=[0])
    return r.results[0]["out_0"]
```

```python
from contextlib import ExitStack

import numpy as np
import concourse.bass as bass
from concourse import mybir

ALU = mybir.AluOpType
ACT = mybir.ActivationFunctionType
AX_X = mybir.AxisListType.X
F32 = mybir.dt.float32
BF16 = mybir.dt.bfloat16
I32 = mybir.dt.int32

NODES, D, EDGES = 6250, 96, 106250
NP, NJ = 125, 2
CN = NP * NJ
CHUNKS = NODES // CN
CW = NJ * D
SPLIT = 120
LANES, TPG = 128, 4
GE = LANES * TPG
SLOTS = 8
HALF = SLOTS // 2
XTILES = HALF * TPG
TURNS = -(-EDGES // (GE * SLOTS))
GROUPS = TURNS * SLOTS
EPAD = GROUPS * GE
PLACE_STEP = 3
TESTED = 19
PAIRS = TURNS // 2
LAG = 3
LATE = 2
DEGREES = SLOTS - 1
WIN = 64
PPASS2 = 7
HALVES2 = 3
GATHER_GROUPS = (PPASS2 - 1) * 2 * SLOTS + HALVES2 * HALF
DT0 = GATHER_GROUPS * TPG
TPU, DWIN = 10, 12
UCOLS = TPU * DWIN
UPP, UPP0, UPPL = 6, 6, 4
UNITS = UPP * (PPASS2 - 2) + UPP0 + UPPL
DTS = UNITS * TPU
UWIN = 96
NA = -(-NODES // LANES)
NA2 = NA + NA % 2
CHALF = NA2 // 2 * DWIN
HOTS = 4
LOOK = HOTS - 1
PARTS = 7
PA = NA // PARTS
STAGES = 3
DCHUNK = 14
TAKING = 3
GWIN = 512
GWINS = -(-NODES // GWIN)
SUMS = GWINS * GWIN
LEFT = [*range(2 * PPASS2 - 4, DCHUNK), *range(DCHUNK + 2 * (PPASS2 - TAKING) - 1, CHUNKS)]
LN_EPS = BN_EPS = 1e-5
NO_NODE = 1 << 20
LOADS = 5
CPL = CHUNKS // LOADS
TPL = CPL * NJ

W_EDGE, W_1, W_2, W_L, W_R = (D * i for i in range(5))
C_B1, C_BL, C_GAMMA, C_BETA, C_EPS = (5 * D + i for i in range(5))
W_COLS = 5 * D + 5

assert (DT0 + DTS) * LANES >= EDGES and PA * PARTS == NA


def graph_layers(nc, x, edge_attr_t, src_blocks, dst_cols, dst_first, dense_src, dense_dst, tile_first,
                 column_first, unit_first, column_offset, weights, identity, out):
    h_dram = nc.dram_tensor("h_rows", [NODES, D], F32).ap()
    h2_padded = nc.dram_tensor("h2_rows", [NA * LANES, D], F32).ap()
    h2_dram = h2_padded[0:NODES, :]

    with ExitStack() as ctx:
        def sb(name, shape, dt=F32):
            return ctx.enter_context(nc.sbuf_tensor(name, shape, dt))

        def sem(name):
            return ctx.enter_context(nc.semaphore(name))

        x_nm = sb("x_nm", [NP, CHUNKS * CW])
        h_or_pre = sb("h_or_pre", [NP, NODES])
        h_nm = h_or_pre[:, 0:CHUNKS * CW]
        l1_fm = h_or_pre[0:D, :]
        h_or_rdeg = sb("h_or_rdeg", [D, NODES])
        sums0_or_h2 = sb("sums0_or_h2", [LANES, NA * 3 * D // 2])
        sums0 = sums0_or_h2[0:D + 1, 0:SUMS]
        h2_parts = sums0_or_h2[:, :].bitcast(BF16).rearrange("b (a q) -> b a q", q=3 * D)
        sums1 = sb("sums1", [D, SUMS])
        w = sb("w", [D + 1, W_COLS])
        ident = sb("ident", [LANES, LANES])
        ones = sb("ones", [LANES, LANES])
        iota = sb("iota", [LANES, GWIN])
        dst_i = sb("dst_i", [LANES, GROUPS * TPG], I32)
        rel = sb("rel", [LANES, GROUPS * TPG])
        base_i = sb("base_i", [LANES, GROUPS], I32)
        ahead = sb("ahead", [LANES, GROUPS])
        idx = sb("idx", [LANES, 4, HALF * TPG], I32)
        edge_buf = sb("edge_buf", [LANES, max(NA2 * UCOLS, HALF * 2 * GE + TPG * GWIN)])
        attr = edge_buf[0:D + 1, 0:HALF * 2 * GE].rearrange("f (q e) -> f q e", q=HALF)
        gsel = edge_buf[:, HALF * 2 * GE:HALF * 2 * GE + TPG * GWIN]
        counts = edge_buf[:, 0:NA2 * UCOLS].bitcast(BF16).rearrange("b (u a n) -> b u a n", u=2, a=NA2)
        gat = sb("gat", [LANES, SLOTS, TPG * D])
        pre = sb("pre", [LANES, 2, TPG * D])
        msg = sb("msg", [LANES, 2, TPG * (D + 1)])
        stage2 = sb("stage2", [LANES, PA * D])
        h2_stage = [t[:, :, :].rearrange("p b n -> p (b n)")[:, 0:PA * D] for t in (pre, msg)] + [stage2[:, :]]
        sel = sb("sel", [LANES, 2, TPG * WIN])
        slack = sb("slack", [LANES, 19])
        ends = sb("ends", [LANES, 8])
        src_i = sb("src_i", [LANES, DTS + LOOK], I32)
        dense_i = sb("dense_i", [LANES, DTS + LOOK], I32)
        src_a = sb("src_a", [LANES, DTS + LOOK])
        src_b = sb("src_b", [LANES, DTS + LOOK])
        column = sb("column", [LANES, DTS + LOOK])
        tile_i = sb("tile_i", [LANES, DTS + LOOK], I32)
        unit_i = sb("unit_i", [LANES, UNITS], I32)
        place_i = sb("place_i", [LANES, UNITS], I32)
        place = sb("place", [LANES, UNITS])
        offset = sb("offset", [LANES, 1])
        iota16 = sb("iota16", [LANES, 2 * CHALF], mybir.dt.float16)
        hot_b = sb("hot_b", [LANES, HOTS, LANES], BF16)
        hot_c = sb("hot_c", [LANES, HOTS, 2 * CHALF], BF16)
        placer = sb("placer", [LANES, UWIN])
        unit_sum = sb("unit_sum", [LANES, 3, D])
        zeros = sb("zeros", [NA * LANES - NODES, D])
        wide_i = sb("wide_i", [1, 1], I32)
        stats = sb("stats", [NP, TPL, 6])
        moments = sb("moments", [NP, 2, 5, TPL])
        sd = sb("sd", [NP, 2, TPL])
        rstd = sb("rstd", [NP, 2, TPL])
        nmr = sb("nmr", [NP, 2, TPL])
        ring_stats = sb("ring_stats", [LANES, XTILES, 6])
        ring_moments = sb("ring_moments", [LANES, 5, XTILES])
        ring_sd, ring_rstd, ring_nmr = (sb(n, [LANES, XTILES]) for n in ("ring_sd", "ring_rstd", "ring_nmr"))
        u = sb("u", [D, CN])
        z = sb("z", [D + 1, CN])
        degrow = sb("degrow", [D + 1, CN])
        h2 = sb("h2", [NP, CW])
        h2t = sb("h2t", [D, CN])
        eps_c = sb("eps_c", [LANES, 1])
        eps1 = sb("eps1", [D + 1, 1])
        bstats = sb("bstats", [D, CHUNKS, 6])
        bmv = sb("bmv", [D, 2])
        bn = sb("bn", [D, 6])

        banks = ctx.enter_context(nc.psum_tensor("banks", [LANES, 8, 512], F32))
        agg_ps = [banks[:, 0, :], banks[:, 1, :]]
        ea_ps = [banks[:, 2, :], banks[:, 3, :]]
        node_ps = [banks[:, b, :] for b in range(4, 8)]
        z_ps, y_ps, t_ps, deg_ps = node_ps
        agg1_ps, l1_ps = banks[:, 0, :], [banks[:, 1, 0:CN], banks[:, 0, 0:CN]]
        unit_ps = [banks[:, 2, :], banks[:, 3, :]]
        placed_ps = [ps[0:D, 3 * D:3 * D + UWIN] for ps in unit_ps]
        count_ps = [banks[:, 4:6, 0:CHALF], banks[:, 6:8, 0:CHALF]]

        mean_fm = [u[:, :], z[0:D, :]]

        def at(start, size):
            return slice(start, start + size) if isinstance(start, int) else bass.ds(start, size)

        def rows_of(rows, c, n=1):
            return rows.rearrange("(c p j) f -> p c (j f)", p=NP, j=NJ)[:, at(c, n), :]

        def chunk_sums(sums, c, rows):
            return sums[rows, at(c * CN, CN)].rearrange("f (p j) -> f j p", j=NJ)

        def blocks_of_h2(i, part):
            return h2_parts[:, i * PA:(i + 1) * PA, part * D:(part + 1) * D]

        def staged(i):
            return h2_stage[i % STAGES].rearrange("b (a f) -> b a f", f=D)

        def tiles(ap):
            return ap.rearrange("f (j p) -> f j p", p=NP)

        rel3 = rel[:, :].rearrange("p (g k) -> p g k", k=TPG)
        sums = [sums0, sums1]
        sum_rows = [D + 1, D]

        x_in = [sem(f"x_in{i}") for i in range(LOADS)]
        w_in, dst_in = sem("w_in"), sem("dst_in")
        consts_set, ones_set, sums_set = sem("consts_set"), sem("ones_set"), sem("sums_set")
        test_step, bad_summed, wide_ready = sem("test_step"), sem("bad_summed"), sem("wide_ready")
        var_done, sd_done, scale_done = sem("var_done"), sem("sd_done"), sem("scale_done")
        h_done, h_out, h_turned = sem("h_done"), sem("h_out"), sem("h_turned")
        h_copied = [sem("h_copied0"), sem("h_copied1")]
        ring_var_done, ring_sd_done, ring_scale_done, ring_done = (
            sem(n) for n in ("ring_var_done", "ring_sd_done", "ring_scale_done", "ring_done"))
        mixed, z_mm, z_done, y_mm, x1_done = (sem(n) for n in ("mixed", "z_mm", "z_done", "y_mm", "x1_done"))
        deg_copied, deg_mm, deg_max, rdeg_done = (
            sem(n) for n in ("deg_copied", "deg_mm", "deg_max", "rdeg_done"))
        var2_done, sd2_done, scale2_done = sem("var2_done"), sem("sd2_done"), sem("scale2_done")
        h2_done, h2_turned, h2_copied = sem("h2_done"), sem("h2_turned"), sem("h2_copied")
        h2_out = sem("h2_out")
        r_mm, r_done = sem("r_mm"), sem("r_done")
        mean_done, l1_mm, l1_done, bstat_done = (
            sem(n) for n in ("mean_done", "l1_mm", "l1_done", "bstat_done"))
        bmv_done, bsd_done, affine_done = sem("bmv_done"), sem("bsd_done"), sem("affine_done")
        y1_done, y1_turned, out_done, stored = (
            sem(n) for n in ("y1_done", "y1_turned", "out_done", "stored"))
        dve_step, node_step = sem("dve_step"), sem("node_step")
        wait_carried = sem("wait_carried")
        group_taken = sem("group_taken")

        dense_in, dense_set = sem("dense_in"), sem("dense_set")
        pad_out = sem("pad_out")
        part_in = [sem(f"part_in{b}") for b in range(STAGES)]
        part_hi, part_rest, part_mid, part_lo = (
            sem(n) for n in ("part_hi", "part_rest", "part_mid", "part_lo"))
        hot_done, counted, count_copied = sem("hot_done"), sem("counted"), sem("count_copied")
        unit_mm, unit_hi, unit_mid, unit_summed = (
            sem(n) for n in ("unit_mm", "unit_hi", "unit_mid", "unit_summed"))
        placer_done, placed, unit_added = sem("placer_done"), sem("placed"), sem("unit_added")

        idx_in = [sem(f"idx_in{b}") for b in range(4)]
        gathered = [sem(f"gathered{s}") for s in range(SLOTS)]
        attr_in = [sem(f"attr_in{q}") for q in range(HALF)]
        ea_done, pre_done, msg_done = sem("ea_done"), sem("pre_done"), sem("msg_done")
        sel_done = [sem(f"sel_done{p}") for p in range(2)]
        agg_done = [sem(f"agg_done{p}") for p in range(2)]
        acc_done = [sem(f"acc_done{p}") for p in range(2)]
        gsel_done = [sem(f"gsel_done{p}") for p in range(2)]
        gagg_done = [sem(f"gagg_done{p}") for p in range(2)]
        gacc_done = [sem(f"gacc_done{p}") for p in range(2)]

        def wait_past(eng, s, i, count):
            if not isinstance(i, int) or count > 0:
                eng.wait_ge(s, count)

        def turns(eng, turn):
            turn(0)
            with eng.Fori(1, TURNS) as i:
                turn(i)

        def left_chunks(steps, rounds):
            for k in rounds:
                for rank, at_slot in enumerate(sorted(steps)):
                    if 0 <= k - rank < len(LEFT):
                        for step in steps[at_slot]:
                            step(LEFT[k - rank], CHUNKS - len(LEFT) + k - rank, (k - rank + 1) % 2)

        def whole_chunk(steps, c, n):
            for s in sorted(steps):
                for step in steps[s]:
                    step(c, n)

        def turns_with_nodes(eng, group, steps, flush=None):
            h2_steps = {k: v for k, v in steps.items() if k != DEGREES}

            def turn(i, taken, steps=steps):
                for s in range(SLOTS):
                    group(i, s)
                    for c, late in taken:
                        for step in steps.get(s - late, ()):
                            step(c, c)
                if flush:
                    flush(i)
            turn(0, [])
            with eng.Fori(1, LAG) as i:
                turn(i, [])
            with eng.Fori(LAG, TURNS - 1) as i:
                turn(i, [(i - LAG, 0)])
            late_chunk = TURNS - LAG
            turn(TURNS - 1, [(late_chunk - 1, 0), (late_chunk, LATE)], h2_steps)
            whole_chunk({k: v for k, v in h2_steps.items() if k + LATE >= SLOTS}, late_chunk, late_chunk)
            for c in range(late_chunk + 1, CHUNKS):
                whole_chunk(h2_steps, c, c)
            for c in range(late_chunk - 1, CHUNKS):
                whole_chunk({DEGREES: steps[DEGREES]}, c, c)

        def turns_then_nodes(eng, group, steps, after_edges=None):
            def turn(i):
                for s in range(SLOTS):
                    group(i, s)
            turns(eng, turn)
            if after_edges:
                after_edges()

            whole_chunk(steps, 0, 0)
            with eng.Fori(1, CHUNKS) as c:
                whole_chunk(steps, c, c)

        def of_pair(j):
            if isinstance(j, int) and j == 0:
                return 0, UPP0
            return UPP * j - (UPP - UPP0), UPPL if isinstance(j, int) and j == PPASS2 - 1 else UPP

        def chunks_of_pair(j):
            if isinstance(j, int) and j < TAKING:
                return [(0, 0), (1, 1)] if j == TAKING - 1 else []
            cs = (2 * j - 4, 2 * j - 3, 2 * j + DCHUNK - 2 * TAKING, 2 * j + DCHUNK - 2 * TAKING + 1)
            if isinstance(j, int) and j == PPASS2 - 1:
                cs = cs[:-1]
            return [(c, 4 * (j - TAKING) + 2 + q) for q, c in enumerate(cs)]

        def pairs_with_dense(eng, group, dense, steps, add_group=None, split=None):
            def pair(j):
                first, units = of_pair(j)
                start, end = (isinstance(j, int) and j == k for k in (0, PPASS2 - 1))
                slots = HALVES2 * HALF if end else 2 * SLOTS
                slot_steps = [[] for _ in range(slots)]
                for n in range(units * TPU):
                    slot_steps[n * slots // (units * TPU)].append((n // TPU, n % TPU))
                added = 0 if start else first - 2
                for s in range(slots):
                    g = j * 2 * SLOTS + s
                    if not start:
                        group(j, s)
                    for k, (u, t) in enumerate(slot_steps[s]):
                        stages = {"build"}
                        if not start or u >= 1:
                            stages.add("multiply")
                        if not start or u >= 2:
                            stages.add("finish")
                        groups_added = max(g - 1, 0) + (k > 0 and g > 0) if start else g + (k > 0)
                        dense(first + u, (u + UPP0 * start) % 2, t, stages, groups_added)
                        if "finish" in stages and t == PLACE_STEP:
                            added = added + 1
                        if k == 0 and add_group and not (start and g == 0):
                            add_group(g - 1 if start else g, added)
                        if split and start and u == 0 and t <= PARTS:
                            split(t)
                    if start:
                        group(j, s)
                    for q, (c, n) in enumerate(chunks_of_pair(j)):
                        for step in steps.get(s - 4 * q, ()):
                            step(c, n)
                if start and add_group:
                    add_group(2 * SLOTS - 1, added)

            for j in range(TAKING):
                pair(j)
            with eng.Fori(TAKING, PPASS2 - 1) as j:
                pair(j)
            pair(PPASS2 - 1)
            rounds = len(LEFT) - 1
            for t in range(TPU):
                dense(UNITS, UPPL % 2, t, {"multiply", "finish"}, GATHER_GROUPS)
                if 1 <= t <= rounds:
                    left_chunks(steps, [t - 1])
            for t in range(PLACE_STEP + 1):
                dense(UNITS + 1, (UPPL + 1) % 2, t, {"finish"}, GATHER_GROUPS)
            left_chunks(steps, [rounds, rounds + 1])

        def hot_buffer(b, t):
            return (b * TPU + t) % HOTS

        def gathers_by(p, i):
            return (p * TURNS + i + 1) * TPG * 16

        block = ctx.enter_context(nc.Block())

        @block.sync
        def _(sp):
            sp.dma_start(idx[:, 0, :], src_blocks[0:1].rearrange("a p k -> (a p) k")).then_inc(idx_in[0], 16)
            for i in range(LOADS):
                sp.dma_start(x_nm[0:SPLIT, i * CPL * CW:(i + 1) * CPL * CW].rearrange("p (c n) -> p c n", n=CW),
                             rows_of(x, i * CPL, CPL)[0:SPLIT]).then_inc(x_in[i], 16)
            sp.dma_start(w[:, :], weights[:, :]).then_inc(w_in, 16)
            sp.dma_start(dst_i[:, :], dst_cols[:, :]).then_inc(dst_in, 16)
            sp.dma_start(base_i[:, :], dst_first.to_broadcast([LANES, GROUPS])).then_inc(dst_in, 16)
            sp.dma_start(src_i[:, :], dense_src[:, :]).then_inc(dense_in, 16)
            sp.dma_start(dense_i[:, :], dense_dst[:, :]).then_inc(dense_in, 16)
            sp.dma_start(tile_i[:, :], tile_first.to_broadcast([LANES, DTS + LOOK])).then_inc(dense_in, 16)
            sp.dma_start(unit_i[:, :], unit_first.to_broadcast([LANES, UNITS])).then_inc(dense_in, 16)
            sp.dma_start(place_i[:, :], column_first[:, :]).then_inc(dense_in, 16)
            sp.dma_start(offset[:, :], column_offset[:, :]).then_inc(dense_in, 16)

            def load_idx(p, j, t, h):
                for s in range(h * HALF, (h + 1) * HALF):
                    wait_past(sp, gathered[s], j, gathers_by(p, 2 * j + t - 2))
                sp.dma_start(idx[:, 2 * t + h, :],
                             src_blocks[at((2 * j + t) * 2 + h, 1)].rearrange("a p k -> (a p) k")
                             ).then_inc(idx_in[2 * t + h], 16)

            def load_turn(j, t, last=False):
                i = 2 * j + t
                for q in range(HALF):
                    if q % 2 == 0:
                        after = (0, j, 1) if t == 0 else (1, 0, 0) if last else (0, j + 1, 0)
                        load_idx(*after, q // 2)
                    wait_past(sp, ea_done, i, (i - 1) * SLOTS + 2 * q + 2)
                    sp.dma_start(attr[0:D, q, :],
                                 edge_attr_t[:, at(i * (SLOTS * GE) + q * 2 * GE, 2 * GE)]
                                 ).then_inc(attr_in[q], 16)

            load_idx(0, 0, 0, 1)
            load_turn(0, 0)
            for i in range(LOADS):
                sp.wait_ge(h_done, TPL * (i + 1))
                for a, b in ((0, SPLIT), (SPLIT, NP)):
                    sp.dma_start(rows_of(h_dram, i * CPL, CPL)[a:b],
                                 h_nm[a:b, i * CPL * CW:(i + 1) * CPL * CW].rearrange("p (c n) -> p c n", n=CW)
                                 ).then_inc(h_out, 16)
            load_turn(0, 1)
            with sp.Fori(1, PAIRS - 1) as j:
                for t in range(2):
                    load_turn(j, t)
            for t in range(2):
                load_turn(PAIRS - 1, t, last=True)

            for h in range(2):
                load_idx(1, 0, 1, h)
            def rest_of_indices(pairs, halves=0):
                with sp.Fori(1, pairs) as j:
                    for t in range(2):
                        for h in range(2):
                            load_idx(1, j, t, h)
                for n in range(halves):
                    load_idx(1, pairs, n // 2, n % 2)

            sp.wait_ge(pad_out, 16)
            sp.wait_ge(wide_ready, 1)
            wide = sp.value_load(wide_i[0:1, 0:1], min_val=0, max_val=LANES)
            with sp.If(wide < 1):
                sp.wait_ge(h2_out, 32 * CHUNKS)
                for i in range(PARTS):
                    if i >= STAGES:
                        sp.wait_ge(part_lo, i - STAGES + 1)
                    sp.dma_start(h2_stage[i % STAGES].rearrange("b (a f) -> b a f", f=D),
                                 h2_padded.rearrange("(a b) f -> b a f", b=LANES)[:, i * PA:(i + 1) * PA, :]
                                 ).then_inc(part_in[i % STAGES], 16)
                rest_of_indices(PPASS2 - 1, HALVES2)
            with sp.Else():
                rest_of_indices(PAIRS)

            for i in range(LOADS):
                sp.wait_ge(out_done, CPL * (i + 1))
                for a, b in ((0, SPLIT), (SPLIT, NP)):
                    sp.dma_start(rows_of(out, i * CPL, CPL)[a:b],
                                 x_nm[a:b, i * CPL * CW:(i + 1) * CPL * CW].rearrange("p (c n) -> p c n", n=CW)
                                 ).then_inc(stored, 16)
            sp.wait_ge(stored, 32 * LOADS)

        @block.gpsimd
        def _(pool):
            nc.gpsimd.iota(iota[:, :], pattern=[[1, GWIN]], base=0, channel_multiplier=0,
                           allow_small_or_imprecise_dtypes=True).then_inc(consts_set, 1)
            nc.gpsimd.iota(iota16[:, :], pattern=[[1, 2 * CHALF]], base=0, channel_multiplier=0,
                           allow_small_or_imprecise_dtypes=True).then_inc(consts_set, 1)

            def gather_half(p, j, t, h, table):
                pool.wait_ge(idx_in[2 * t + h], 16 * (p * PAIRS + j + 1))
                for s in range(h * HALF, (h + 1) * HALF):
                    wait_past(pool, pre_done if p == 0 else agg_done[1], j, (2 * j + t - 1) * SLOTS + s + 1)
                    pool.sem_inc(group_taken, 1)
                    for k in range(TPG):
                        col = (s % HALF) * TPG + k
                        nc.gpsimd.indirect_dma_start(
                            out=gat[:, s, k * D:(k + 1) * D], out_offset=None, in_=table[:, :],
                            in_offset=bass.IndirectOffsetOnAxis(
                                ap=idx[:, 2 * t + h, col:col + 1], axis=0),
                        ).then_inc(gathered[s], 16)

            HALVES = [(0, 0), (0, 1), (1, 0), (1, 1)]

            def loop_of_pairs(p, table, n):
                with pool.Fori(1, n) as j:
                    for t, h in HALVES:
                        gather_half(p, j, t, h, table)

            gather_half(0, 0, 0, 0, x)
            nc.gpsimd.memset(sums0[:, :], 0.0).then_inc(sums_set, 1)
            nc.gpsimd.memset(zeros[:, :], 0.0).then_inc(sums_set, 1)
            nc.gpsimd.memset(sums1[:, :], 0.0).then_inc(sums_set, 1)

            pool.wait_ge(h_out, 32 * LOADS)
            for t, h in HALVES[1:]:
                gather_half(0, 0, t, h, h_dram)
            loop_of_pairs(0, h_dram, PAIRS)
            pool.wait_ge(wide_ready, 1)
            pool.wait_ge(h2_out, 32 * CHUNKS)
            wide = pool.value_load(wide_i[0:1, 0:1], min_val=0, max_val=LANES)
            for t, h in HALVES:
                gather_half(1, 0, t, h, h2_dram)
            with pool.If(wide < 1):
                loop_of_pairs(1, h2_dram, PPASS2 - 1)
                for t, h in HALVES[:HALVES2]:
                    gather_half(1, PPASS2 - 1, t, h, h2_dram)
            with pool.Else():
                loop_of_pairs(1, h2_dram, PAIRS)

        @block.tensor
        def _(pe):
            pe.wait_ge(w_in, 32)
            for c in range(CHUNKS):
                pe.wait_ge(h_done, NJ * (c + 1))
                if c >= 4:
                    pe.wait_ge(h_copied[c % 2], (c - 4) // 2 + 1)
                for j in range(NJ):
                    mm = nc.tensor.transpose(node_ps[c % 4][0:D, j * NP:(j + 1) * NP],
                                             h_nm[:, (c * NJ + j) * D:(c * NJ + j + 1) * D],
                                             ident[0:NP, 0:NP])
                mm.then_inc(h_turned, 1)

            pe.wait_ge(ones_set, 3)
            pe.wait_ge(test_step, TESTED)
            nc.tensor.matmul(agg_ps[0][0:1, 0:1], slack[:, 15:16], ones[:, 0:1],
                             start=True, stop=True).then_inc(bad_summed, 1)
            pe.wait_ge(wide_ready, 1)
            wide = pe.value_load(wide_i[0:1, 0:1], min_val=0, max_val=LANES)

            def edge_products(i, s):
                if s % 2 == 0:
                    pe.wait_ge(attr_in[s // 2], 16 * (i + 1))
                wait_past(pe, pre_done, i, i * SLOTS + s - 1)
                for k in range(TPG):
                    a = (s % 2) * GE + k * LANES
                    mm = nc.tensor.matmul(ea_ps[s % 2][:, k * D:(k + 1) * D],
                                          attr[:, s // 2, a:a + LANES],
                                          w[:, W_EDGE:W_EDGE + D], start=True, stop=True)
                mm.then_inc(ea_done, 1)

            def messages(p, s, k):
                if p == 0:
                    return msg[:, s % 2, k * (D + 1):(k + 1) * (D + 1)]
                return gat[:, s, k * D:(k + 1) * D]

            def messages_ready(p, i, s):
                if p == 0:
                    pe.wait_ge(msg_done, i * SLOTS + s + 1)
                else:
                    pe.wait_ge(gathered[s], gathers_by(1, i))

            def sum_group(p, i, s):
                messages_ready(p, i, s)
                pe.wait_ge(sel_done[p], i * SLOTS + s + 1)
                wait_past(pe, acc_done[p], i, i * SLOTS + s - 1)
                for k in range(TPG):
                    mm = nc.tensor.matmul(agg_ps[s % 2][0:sum_rows[p], 0:WIN], messages(p, s, k),
                                          sel[:, s % 2, k * WIN:(k + 1) * WIN],
                                          start=(k == 0), stop=(k == TPG - 1))
                mm.then_inc(agg_done[p], 1)

            def sum_group_general(p, i, s):
                messages_ready(p, i, s)
                for v in range(GWINS):
                    n = (i * SLOTS + s) * GWINS + v
                    pe.wait_ge(gsel_done[p], n + 1)
                    wait_past(pe, gacc_done[p], i, n)
                    for k in range(TPG):
                        mm = nc.tensor.matmul(agg_ps[0][0:sum_rows[p], :], messages(p, s, k),
                                              gsel[:, k * GWIN:(k + 1) * GWIN],
                                              start=(k == 0), stop=(k == TPG - 1))
                    mm.then_inc(gagg_done[p], 1)
                pe.wait_ge(gacc_done[p], (i * SLOTS + s + 1) * GWINS)
                pe.nop().then_inc(agg_done[p], 1)

            def first_product(c, n):
                pe.wait_ge(mixed, n + 1)
                wait_past(pe, z_done, n, n)
                nc.tensor.matmul(z_ps[0:D, 0:CN], w[0:D, W_1:W_1 + D], u[:, :],
                                 start=True, stop=True).then_inc(z_mm, 1)

            def spread_degrees(c, n):
                pe.wait_ge(deg_copied, n + 1)
                wait_past(pe, deg_max, n, n)
                nc.tensor.matmul(deg_ps[0:D, 0:CN], ones[D:D + 1, 0:D], degrow[D:D + 1, :],
                                 start=True, stop=True).then_inc(deg_mm, 1)

            def second_product(c, n):
                pe.wait_ge(z_done, n + 1)
                wait_past(pe, x1_done, n, n)
                for j in range(NJ):
                    mm = nc.tensor.matmul(y_ps[0:NP, j * D:(j + 1) * D], z[:, j * NP:(j + 1) * NP],
                                          w[:, W_2:W_2 + D], start=True, stop=True)
                mm.then_inc(y_mm, 1)

            def turn_h2(c, n):
                pe.wait_ge(h2_done, n + 1)
                wait_past(pe, r_done, n, n)
                for j in range(NJ):
                    mm = nc.tensor.transpose(t_ps[0:D, j * NP:(j + 1) * NP],
                                             h2[:, j * D:(j + 1) * D], ident[0:NP, 0:NP])
                mm.then_inc(h2_turned, 1)

            def root_product(c, n):
                pe.wait_ge(h2_copied, n + 1)
                nc.tensor.matmul(t_ps[0:D, CN:2 * CN], w[0:D, W_R:W_R + D], h2t[:, :],
                                 start=True, stop=True).then_inc(r_mm, 1)

            def mean_product(c, n, b=None):
                pe.wait_ge(mean_done, n + 1)
                wait_past(pe, l1_done, n, n if b is None else n - 1)
                if b == 1:
                    pe.wait_ge(acc_done[1], GATHER_GROUPS)
                nc.tensor.matmul(l1_ps[b or 0][0:D, :], w[0:D, W_L:W_L + D], mean_fm[b or 0],
                                 start=True, stop=True).then_inc(l1_mm, 1)

            def gathered_group1(j, s):
                g = j * (2 * SLOTS) + s
                pe.wait_ge(gathered[s % SLOTS], gathers_by(1, 2 * j + s // SLOTS))
                pe.wait_ge(sel_done[1], g + 1)
                wait_past(pe, acc_done[1], g, g)
                for k in range(TPG):
                    mm = nc.tensor.matmul(agg1_ps[0:D, 0:WIN], messages(1, s % SLOTS, k),
                                          sel[:, s % 2, k * WIN:(k + 1) * WIN],
                                          start=(k == 0), stop=(k == TPG - 1))
                mm.then_inc(agg_done[1], 1)

            def dense(v, b, t, stages, groups_added):
                if "build" in stages:
                    tile = v * TPU + t
                    pe.wait_ge(hot_done, tile + 1)
                    wait_past(pe, count_copied, v, tile - 1)
                    for q in range(2):
                        mm = nc.tensor.matmul(count_ps[t % 2][:, q, :], hot_b[:, hot_buffer(b, t), :],
                                              hot_c[:, hot_buffer(b, t), q * CHALF:(q + 1) * CHALF],
                                              start=True, stop=True)
                    mm.then_inc(counted, 1)
                if "multiply" in stages:
                    if t == 0:
                        pe.wait_ge(count_copied, v * TPU)
                        wait_past(pe, unit_added, v, v - 2)
                        if isinstance(v, int) and v == 1:
                            pe.wait_ge(part_lo, PARTS)
                    for a in range(NA * t // TPU, NA * (t + 1) // TPU):
                        mm = nc.tensor.matmul(unit_ps[1 - b][0:UCOLS, 0:3 * D], counts[:, 1 - b, a, :],
                                              h2_parts[:, a, :], start=(a == 0), stop=(a == NA - 1))
                    if t == TPU - 1:
                        mm.then_inc(unit_mm, 1)
                if "finish" in stages and t == PLACE_STEP:
                    pe.wait_ge(unit_summed, v - 1)
                    pe.wait_ge(placer_done, v - 1)
                    nc.tensor.matmul(placed_ps[b], unit_sum[0:UCOLS, 2, :], placer[0:UCOLS, :],
                                     start=True, stop=True).then_inc(placed, 1)

            steps0 = {1: [first_product], 2: [second_product], 5: [turn_h2], 6: [root_product],
                      DEGREES: [spread_degrees]}
            steps1 = {2: [mean_product]}

            def group0(i, s):
                edge_products(i, s)
                if s > 0:
                    sum_group(0, i, s - 1)

            def group0_general(i, s):
                edge_products(i, s)
                sum_group_general(0, i, s)

            with pe.If(wide < 1):
                turns_with_nodes(pe, group0, steps0, lambda i: sum_group(0, i, SLOTS - 1))
            with pe.Else():
                turns_then_nodes(pe, group0_general, steps0)
            with pe.If(wide < 1):
                pairs_with_dense(pe, gathered_group1, dense, steps1)
            with pe.Else():
                turns_then_nodes(pe, lambda i, s: sum_group_general(1, i, s), steps1)

            for c in range(CHUNKS):
                pe.wait_ge(y1_done, c // 2 + 1)
                if c >= 4:
                    pe.wait_ge(out_done, c - 3)
                for j in range(NJ):
                    a = c * CN + j * NP
                    mm = nc.tensor.transpose(node_ps[c % 4][0:NP, j * D:(j + 1) * D],
                                             l1_fm[:, a:a + NP], ident[0:D, 0:D])
                mm.then_inc(y1_turned, 1)

        @block.scalar
        def _(act):
            for i in range(LOADS):
                act.dma_start(x_nm[SPLIT:NP, i * CPL * CW:(i + 1) * CPL * CW].rearrange("p (c n) -> p c n", n=CW),
                              rows_of(x, i * CPL, CPL)[SPLIT:NP]).then_inc(x_in[i], 16)
            act.dma_start(ident[:, :], identity[:, :]).then_inc(w_in, 16)

            act.wait_ge(ones_set, 1)

            def sd_of_rows(i):
                act.wait_ge(var_done, i + 1)
                if i >= 2:
                    act.wait_ge(scale_done, i - 1)
                nc.scalar.activation(sd[:, i % 2, :], moments[:, i % 2, 4, :], ACT.Sqrt, scale=1.0 / D,
                                     bias=eps_c[0:NP, :]).then_inc(sd_done, 1)

            sd_of_rows(0)
            for i in range(LOADS):
                if i + 1 < LOADS:
                    sd_of_rows(i + 1)
                act.wait_ge(scale_done, i + 1)
                for t in range(TPL):
                    a = (i * TPL + t) * D
                    nc.scalar.activation(h_nm[:, a:a + D], x_nm[:, a:a + D], ACT.Relu,
                                         bias=nmr[:, i % 2, t:t + 1], scale=rstd[:, i % 2, t:t + 1]
                                         ).then_inc(h_done, 1)

            act.wait_ge(ring_var_done, 1)
            nc.scalar.activation(ring_sd[:, :], ring_moments[:, 4, :], ACT.Sqrt, scale=1.0 / D,
                                 bias=eps_c[:, :]).then_inc(ring_sd_done, 1)
            act.wait_ge(ring_scale_done, 1)
            for s in range(HALF):
                for k in range(TPG):
                    t = s * TPG + k
                    rows = gat[:, s, k * D:(k + 1) * D]
                    nc.scalar.activation(rows, rows, ACT.Relu, bias=ring_nmr[:, t:t + 1],
                                         scale=ring_rstd[:, t:t + 1]).then_inc(ring_done, 1)

            for c in range(1, CHUNKS, 2):
                act.wait_ge(h_turned, c + 1)
                nc.scalar.activation(h_or_rdeg[:, c * CN:(c + 1) * CN], node_ps[c % 4][0:D, 0:CN],
                                     ACT.Identity).then_inc(h_copied[1], 1)

            act.wait_ge(ones_set, 5)
            act.wait_ge(wide_ready, 1)
            wide = act.value_load(wide_i[0:1, 0:1], min_val=0, max_val=LANES)

            def relu_messages(i, s):
                act.wait_ge(pre_done, i * SLOTS + s + 1)
                wait_past(act, agg_done[0], i, i * SLOTS + s - 1)
                nc.scalar.activation(
                    msg[:, s % 2, :].rearrange("p (k f) -> p k f", f=D + 1)[:, :, 0:D],
                    pre[:, s % 2, :].rearrange("p (k f) -> p k f", f=D), ACT.Relu).then_inc(msg_done, 1)

            def relu_z(c, n):
                act.wait_ge(z_mm, n + 1)
                wait_past(act, y_mm, n, n)
                nc.scalar.activation(z[0:D, :], z_ps[0:D, 0:CN], ACT.Relu,
                                     bias=w[0:D, C_B1:C_B1 + 1]).then_inc(z_done, 1)

            def copy_degrees(c, n):
                act.wait_ge(mixed, n + 1)
                wait_past(act, deg_mm, n, n)
                nc.scalar.activation(tiles(degrow[D:D + 1, :]), chunk_sums(sums0, c, slice(D, D + 1)),
                                     ACT.Identity).then_inc(deg_copied, 1)

            def sd_h2(c, n):
                act.wait_ge(var2_done, n + 1)
                nc.scalar.activation(sd[:, 0, 0:NJ], moments[:, 0, 4, 0:NJ], ACT.Sqrt, scale=1.0 / D,
                                     bias=eps_c[0:NP, :]).then_inc(sd2_done, 1)

            def relu_h2(c, n):
                act.wait_ge(scale2_done, n + 1)
                wait_past(act, h2_turned, n, n)
                wait_past(act, h2_out, c, 32 * c)
                for j in range(NJ):
                    ins = nc.scalar.activation(h2[:, j * D:(j + 1) * D], x_nm[:, at(c * CW + j * D, D)],
                                               ACT.Relu, bias=nmr[:, 0, j:j + 1], scale=rstd[:, 0, j:j + 1])
                ins.then_inc(h2_done, 1)
                act.wait_ge(h2_done, n + 1)
                for a, b in ((0, SPLIT), (SPLIT, NP)):
                    act.dma_start(rows_of(h2_dram, c)[a:b].rearrange("p c n -> p (c n)"),
                                  h2[a:b, :]).then_inc(h2_out, 16)

            def copy_h2(c, n):
                act.wait_ge(h2_turned, n + 1)
                wait_past(act, r_mm, n, n)
                nc.scalar.activation(h2t[:, :], t_ps[0:D, 0:CN], ACT.Identity).then_inc(h2_copied, 1)

            def root_bias(c, n):
                act.wait_ge(r_mm, n + 1)
                nc.scalar.activation(l1_fm[:, at(c * CN, CN)], t_ps[0:D, CN:2 * CN], ACT.Identity,
                                     bias=w[0:D, C_BL:C_BL + 1]).then_inc(r_done, 1)

            act.wait_ge(h_out, 32 * LOADS)
            act.wait_ge(h_turned, CHUNKS)
            act.wait_ge(sums_set, 2)
            act.dma_start(h2_padded[NODES:NA * LANES, :], zeros[:, :]).then_inc(pad_out, 16)
            steps0 = {1: [relu_z], 3: [sd_h2], 4: [relu_h2], 5: [copy_h2], 6: [root_bias],
                      DEGREES: [copy_degrees]}
            with act.If(wide < 1):
                turns_with_nodes(act, relu_messages, steps0)
            with act.Else():
                turns_then_nodes(act, relu_messages, steps0)

            def dense(v, b, t, stages, groups_added):
                if "build" in stages:
                    act.wait_ge(counted, v * TPU + t + 1)
                    if t == 0:
                        wait_past(act, unit_mm, v, v - 1)
                    nc.scalar.activation(
                        counts[:, b, :, t * DWIN:(t + 1) * DWIN].rearrange("b (q a) d -> b q a d", q=2),
                        count_ps[t % 2].rearrange("b q (a d) -> b q a d", d=DWIN),
                        ACT.Identity).then_inc(count_copied, 1)
                if "finish" in stages and t == 0:
                    act.wait_ge(unit_mm, v - 1)
                    wait_past(act, unit_summed, v, v - 2)
                    nc.scalar.activation(unit_sum[0:UCOLS, 0, :], unit_ps[b][0:UCOLS, 0:D],
                                         ACT.Identity).then_inc(unit_hi, 1)

            def split(i):
                if i < PARTS:
                    act.wait_ge(part_in[i % STAGES], 16 * (i // STAGES + 1))
                    nc.scalar.activation(blocks_of_h2(i, 0), staged(i), ACT.Identity).then_inc(part_hi, 1)
                if i > 0:
                    act.wait_ge(part_rest, i)
                    nc.scalar.activation(blocks_of_h2(i - 1, 1), staged(i - 1), ACT.Identity).then_inc(part_mid, 1)

            with act.If(wide < 1):
                pairs_with_dense(act, lambda j, s: None, dense, {}, split=split)

            act.wait_ge(bmv_done, 1)
            nc.scalar.activation(bn[:, 0:1], bmv[:, 1:2], ACT.Sqrt, bias=eps_c[0:D, :]).then_inc(bsd_done, 1)
            act.wait_ge(affine_done, 1)
            for c in range(0, CHUNKS, 2):
                part = l1_fm[:, c * CN:min(c + 2, CHUNKS) * CN]
                nc.scalar.activation(part, part, ACT.Relu, bias=bn[:, 4:5], scale=bn[:, 2:3]
                                     ).then_inc(y1_done, 1)

        @block.vector
        def _(dve):
            nc.vector.memset(eps_c[:, :], LN_EPS).then_inc(ones_set, 1)
            nc.vector.memset(ones[:, :], 1.0).then_inc(ones_set, 1)
            nc.vector.memset(attr[D:D + 1, :, :], 1.0).then_inc(ones_set, 1)
            nc.vector.memset(z[D:D + 1, :], 1.0).then_inc(ones_set, 1)
            nc.vector.memset(msg[:, :, :], 1.0).then_inc(ones_set, 1)

            dve_steps = [0]

            def in_order(ins):
                dve_steps[0] += 1
                ins.then_inc(dve_step, 1)
                dve.wait_ge(dve_step, dve_steps[0])

            def sums_of_means(st, mo):
                mean_e, m2_e, mean_o, m2_o = (st[:, :, f] for f in (1, 2, 4, 5))
                nc.vector.tensor_tensor(mo[:, 0, :], mean_e, mean_o, ALU.add)
                nc.vector.tensor_tensor(mo[:, 2, :], m2_e, m2_o, ALU.add)
                return nc.vector.tensor_tensor(mo[:, 1, :], mean_e, mean_o, ALU.subtract)

            def squared_difference(mo):
                return nc.vector.tensor_tensor(mo[:, 3, :], mo[:, 1, :], mo[:, 1, :], ALU.mult)

            def d_times_variance(mo):
                return nc.vector.scalar_tensor_tensor(out=mo[:, 4, :], in0=mo[:, 3, :], scalar=D / 4.0,
                                                      in1=mo[:, 2, :], op0=ALU.mult, op1=ALU.add)

            def minus_mean_rstd(out, mo, r):
                return nc.vector.scalar_tensor_tensor(out=out, in0=mo[:, 0, :], scalar=-0.5, in1=r,
                                                      op0=ALU.mult, op1=ALU.mult)

            def stats_of_rows(i):
                dve.wait_ge(x_in[i], 32)
                for t in range(TPL):
                    a = (i * TPL + t) * D
                    ins = nc.vector.bn_stats(stats[:, t, :], x_nm[:, a:a + D])
                in_order(ins)
                mo = moments[:, i % 2]
                in_order(sums_of_means(stats, mo))
                in_order(squared_difference(mo))
                d_times_variance(mo).then_inc(var_done, 1)

            def tested(ins):
                ins.then_inc(test_step, 1)
                tests[0] += 1
                dve.wait_ge(test_step, tests[0])

            tests = [0]
            full, part = EDGES // LANES, EDGES % LANES

            def test_dense_tiles():
                dve.wait_ge(dst_in, 32)
                dve.wait_ge(dense_in, 96)
                dve.wait_ge(consts_set, 2)
                tested(nc.vector.tensor_tensor(column[:, :], dense_i[:, :], tile_i[:, :], ALU.subtract))
                nc.vector.tensor_scalar(dense_i[:, :], src_i[:, :], LANES.bit_length() - 1, None,
                                        ALU.logical_shift_right)
                lo, hi = slack[:, 4:5], slack[:, 16:17]
                nc.vector.tensor_reduce(lo, column[:, 0:full - DT0], AX_X, ALU.min)
                tested(nc.vector.tensor_reduce(hi, column[:, 0:full - DT0], AX_X, ALU.max))
                last = column[0:part, full - DT0:full - DT0 + 1]
                nc.vector.tensor_tensor(slack[0:part, 4:5], slack[0:part, 4:5], last, ALU.min)
                tested(nc.vector.tensor_tensor(slack[0:part, 16:17], slack[0:part, 16:17], last, ALU.max))
                nc.vector.tensor_scalar(slack[:, 5:6], hi, -1.0, float(DWIN - 1), ALU.mult, ALU.add)
                nc.vector.tensor_scalar(src_i[:, :], src_i[:, :], LANES - 1, None, ALU.bitwise_and)
                tested(nc.vector.tensor_scalar(src_a[:, :], dense_i[:, :], float(DWIN), None, ALU.mult))
                nc.vector.tensor_copy(src_b[:, :], src_i[:, :])
                tested(nc.vector.tensor_tensor(column[:, :], column[:, :], src_a[:, :], ALU.add))
                tested(nc.vector.tensor_tensor(place[:, :], place_i[:, :], unit_i[:, :], ALU.subtract))
                nc.vector.tensor_reduce(slack[:, 6:7], place[:, :], AX_X, ALU.min)
                tested(nc.vector.tensor_reduce(slack[:, 17:18], place[:, :], AX_X, ALU.max))
                nc.vector.tensor_scalar(slack[:, 7:8], slack[:, 17:18], -1.0, float(UWIN - DWIN), ALU.mult, ALU.add)
                tested(nc.vector.tensor_scalar(place[:, :], place[:, :], offset[:, 0:1], None, ALU.add))

            def test_groups():
                tested(nc.vector.tensor_tensor(rel3, dst_i[:, :].rearrange("p (g k) -> p g k", k=TPG),
                                               base_i[:, :].unsqueeze(2).to_broadcast([LANES, GROUPS, TPG]),
                                               ALU.subtract))
                tested(nc.vector.tensor_tensor(ahead[:, 1:GROUPS], base_i[:, 1:GROUPS], base_i[:, 0:GROUPS - 1],
                                               ALU.subtract))
                nc.vector.tensor_reduce(slack[:, 0:1], rel[:, 0:full], AX_X, ALU.min)
                nc.vector.tensor_reduce(slack[:, 18:19], rel[:, 0:full], AX_X, ALU.max)
                tested(nc.vector.tensor_reduce(slack[:, 2:3], ahead[:, 1:GROUPS], AX_X, ALU.min))
                nc.vector.tensor_tensor(slack[0:part, 0:1], slack[0:part, 0:1], rel[0:part, full:full + 1], ALU.min)
                nc.vector.tensor_tensor(slack[0:part, 18:19], slack[0:part, 18:19], rel[0:part, full:full + 1],
                                        ALU.max)

            def test_order():
                taken = TURNS - LAG
                tested(nc.vector.scalar_tensor_tensor(
                    out=ahead[:, 0:taken], in0=iota[:, 0:taken], scalar=-float(CN),
                    in1=base_i[:, LAG * SLOTS::SLOTS], op0=ALU.mult, op1=ALU.add))
                nc.vector.tensor_scalar(slack[:, 1:2], slack[:, 18:19], -1.0, float(WIN - 1), ALU.mult, ALU.add)
                tested(nc.vector.tensor_reduce(ends[:, 0:1], ahead[:, 0:taken], AX_X, ALU.min))
                nc.vector.tensor_scalar(slack[:, 3:4], ends[:, 0:1], -float(CN), None, ALU.add)
                nc.vector.tensor_scalar(slack[:, 8:9], base_i[:, GATHER_GROUPS - 1:GATHER_GROUPS], -1.0,
                                        float(DCHUNK * CN - WIN), ALU.mult, ALU.add)
                nc.vector.tensor_tensor(ahead[:, GROUPS - UNITS + 1:GROUPS], unit_i[:, 1:UNITS],
                                        unit_i[:, 0:UNITS - 1], ALU.subtract)
                pairs_taking = PPASS2 - TAKING
                tested(nc.vector.scalar_tensor_tensor(
                    out=ahead[:, 0:pairs_taking], in0=iota[:, 0:pairs_taking], scalar=-2.0 * CN,
                    in1=unit_i[:, of_pair(TAKING)[0] - 2::UPP][:, 0:pairs_taking], op0=ALU.mult, op1=ALU.add))
                nc.vector.tensor_reduce(slack[:, 10:11], ahead[:, GROUPS - UNITS + 1:GROUPS], AX_X, ALU.min)
                tested(nc.vector.tensor_reduce(ends[:, 1:2], ahead[:, 0:pairs_taking], AX_X, ALU.min))
                tested(nc.vector.tensor_scalar(slack[:, 9:10], ends[:, 1:2], -float((DCHUNK + 2) * CN), None,
                                               ALU.add))
                nc.vector.tensor_scalar(slack[:, 11:12], base_i[:, GROUPS - SLOTS + LATE:GROUPS - SLOTS + LATE + 1],
                                        -float((TURNS - LAG + 1) * CN), None, ALU.add)
                tested(nc.vector.tensor_scalar(slack[:, 12:13], unit_i[:, UNITS - 1:UNITS],
                                               -float((CHUNKS - 1) * CN), None, ALU.add))
                tested(nc.vector.tensor_reduce(slack[:, 13:14], slack[:, 0:13], AX_X, ALU.min))
                nc.vector.tensor_scalar(slack[:, 15:16], slack[:, 13:14], 0.0, None, ALU.is_lt).then_inc(test_step, 1)
                assert tests[0] + 1 == TESTED

            stats_of_rows(0)
            for i in range(LOADS):
                if i + 1 < LOADS:
                    stats_of_rows(i + 1)
                if i == LOADS - 1:
                    test_dense_tiles()
                dve.wait_ge(sd_done, i + 1)
                if i >= 2:
                    dve.wait_ge(h_done, TPL * (i - 1))
                in_order(nc.vector.reciprocal(rstd[:, i % 2, :], sd[:, i % 2, :]))
                minus_mean_rstd(nmr[:, i % 2, :], moments[:, i % 2], rstd[:, i % 2, :]).then_inc(scale_done, 1)

            for s in range(HALF):
                dve.wait_ge(gathered[s], gathers_by(0, 0))
                for k in range(TPG):
                    ins = nc.vector.bn_stats(ring_stats[:, s * TPG + k, :], gat[:, s, k * D:(k + 1) * D])
            in_order(ins)
            in_order(sums_of_means(ring_stats, ring_moments))
            in_order(squared_difference(ring_moments))
            d_times_variance(ring_moments).then_inc(ring_var_done, 1)
            test_groups()
            dve.wait_ge(ring_sd_done, 1)
            in_order(nc.vector.reciprocal(ring_rstd[:, :], ring_sd[:, :]))
            minus_mean_rstd(ring_nmr[:, :], ring_moments, ring_rstd[:, :]).then_inc(ring_scale_done, 1)

            test_order()

            for c in range(0, CHUNKS, 2):
                dve.wait_ge(h_turned, c + 1)
                nc.vector.tensor_copy(h_or_rdeg[:, c * CN:(c + 1) * CN], node_ps[c % 4][0:D, 0:CN]
                                      ).then_inc(h_copied[0], 1)
            dve.wait_ge(bad_summed, 1)
            nc.vector.tensor_copy(wide_i[0:1, 0:1], agg_ps[0][0:1, 0:1]).then_inc(wide_ready, 1)
            dve.wait_ge(wide_ready, 1)
            wide = dve.value_load(wide_i[0:1, 0:1], min_val=0, max_val=LANES)
            dve.wait_ge(w_in, 32)
            in_order(nc.vector.tensor_scalar(eps1[:, :], w[:, C_EPS:C_EPS + 1], 1.0, None, ALU.add))
            dve.wait_ge(h_copied[0], CHUNKS - CHUNKS // 2)
            dve.wait_ge(h_copied[1], CHUNKS // 2)

            dve.wait_ge(sums_set, 3)

            def add_gathered(i, s):
                dve.wait_ge(ea_done, i * SLOTS + s + 1)
                if isinstance(i, int) and i == 0 and s < HALF:
                    dve.wait_ge(ring_done, TPG * (s + 1))
                else:
                    dve.wait_ge(gathered[s], gathers_by(0, i))
                wait_past(dve, msg_done, i, i * SLOTS + s - 1)
                nc.vector.tensor_tensor(pre[:, s % 2, :], ea_ps[s % 2][:, 0:TPG * D], gat[:, s, :],
                                        ALU.add).then_inc(pre_done, 1)

            def select(p, i, s):
                wait_past(dve, agg_done[p], i, i * SLOTS + s - 1)
                r = rel[:, at((i * SLOTS + s) * TPG, TPG)]
                nc.vector.tensor_tensor(
                    sel[:, s % 2, :].rearrange("p (k n) -> p k n", n=WIN),
                    iota[:, 0:WIN].unsqueeze(1).to_broadcast([LANES, TPG, WIN]),
                    r.unsqueeze(2).to_broadcast([LANES, TPG, WIN]),
                    ALU.is_equal).then_inc(sel_done[p], 1)

            def add_group(p, i, s):
                g = i * SLOTS + s
                dve.wait_ge(agg_done[p], g + 1)
                start = dve.value_load(base_i[0:1, at(g, 1)], min_val=0, max_val=NODES - 1)
                window = sums[p][0:sum_rows[p], bass.ds(start, WIN)]
                wait_past(dve, acc_done[p], i, g)
                nc.vector.tensor_tensor(window, window, agg_ps[s % 2][0:sum_rows[p], 0:WIN],
                                        ALU.add).then_inc(acc_done[p], 1)

            def group(p):
                def of_slot(i, s):
                    select(p, i, s)
                    if p == 0:
                        add_gathered(i, s)
                    if s > 0:
                        add_group(p, i, s - 1)
                return of_slot

            def group_general(p):
                def of_slot(i, s):
                    if p == 0:
                        add_gathered(i, s)
                    g = i * SLOTS + s
                    first = isinstance(i, int) and g == 0
                    d = dst_i[:, at(g * TPG, TPG)]
                    for v in range(GWINS):
                        n = g * GWINS + v
                        if v > 0 or not first:
                            dve.wait_ge(gagg_done[p], n)
                        nc.vector.scalar_tensor_tensor(
                            out=gsel[:, :].rearrange("p (k n) -> p k n", n=GWIN),
                            in0=iota[:, :].unsqueeze(1).to_broadcast([LANES, TPG, GWIN]),
                            scalar=float(v * GWIN),
                            in1=d.unsqueeze(2).to_broadcast([LANES, TPG, GWIN]),
                            op0=ALU.add, op1=ALU.is_equal).then_inc(gsel_done[p], 1)
                        dve.wait_ge(gagg_done[p], n + 1)
                        if v > 0 or not first:
                            dve.wait_ge(gacc_done[p], n)
                        part = sums[p][0:sum_rows[p], v * GWIN:(v + 1) * GWIN]
                        nc.vector.tensor_tensor(part, part, agg_ps[0][0:sum_rows[p], :],
                                                ALU.add).then_inc(gacc_done[p], 1)
                return of_slot

            def mix(c, n):
                wait_past(dve, z_mm, n, n)
                nc.vector.scalar_tensor_tensor(
                    out=tiles(u[:, :]), in0=tiles(h_or_rdeg[:, at(c * CN, CN)]), scalar=eps1[0:D, :],
                    in1=chunk_sums(sums0, c, slice(0, D)), op0=ALU.mult, op1=ALU.add).then_inc(mixed, 1)

            def clamp_degrees(c, n):
                dve.wait_ge(deg_mm, n + 1)
                dve.wait_ge(mixed, n + 1)
                nc.vector.tensor_scalar(h_or_rdeg[:, at(c * CN, CN)], deg_ps[0:D, 0:CN], 1.0, None,
                                        ALU.max).then_inc(deg_max, 1)

            def invert_degrees(c, n):
                dve.wait_ge(deg_max, n + 1)
                carry_wait()
                part = h_or_rdeg[:, at(c * CN, CN)]
                nc.vector.reciprocal(part, part).then_inc(rdeg_done, 1)

            def residual(c, n):
                dve.wait_ge(y_mm, n + 1)
                part = x_nm[:, at(c * CW, CW)]
                nc.vector.tensor_tensor(part, part, y_ps[0:NP, 0:CW], ALU.add).then_inc(x1_done, 1)

            def carry_wait():
                dve.sem_inc(wait_carried, 1)

            NODE_STEPS = 4
            chunk_moments = moments[:, 0, :, 0:NJ]

            def h2_stats(c, n):
                dve.wait_ge(x1_done, n + 1)
                wait_past(dve, h2_done, n, n)
                carry_wait()
                for j in range(NJ):
                    ins = nc.vector.bn_stats(stats[:, j, :], x_nm[:, at(c * CW + j * D, D)])
                ins.then_inc(node_step, 1)
                dve.wait_ge(node_step, n * NODE_STEPS + 1)
                sums_of_means(stats[:, 0:NJ], chunk_moments).then_inc(node_step, 1)
                dve.wait_ge(node_step, n * NODE_STEPS + 2)
                squared_difference(chunk_moments).then_inc(node_step, 1)
                dve.wait_ge(node_step, n * NODE_STEPS + 3)
                d_times_variance(chunk_moments).then_inc(var2_done, 1)

            def h2_scales(c, n):
                dve.wait_ge(sd2_done, n + 1)
                nc.vector.reciprocal(rstd[:, 0, 0:NJ], sd[:, 0, 0:NJ]).then_inc(node_step, 1)
                dve.wait_ge(node_step, n * NODE_STEPS + 4)
                minus_mean_rstd(nmr[:, 0, 0:NJ], chunk_moments, rstd[:, 0, 0:NJ]).then_inc(scale2_done, 1)

            def mean(c, n, b=None):
                wait_past(dve, l1_mm, n, n if b is None else n - 1)
                nc.vector.tensor_tensor(tiles(mean_fm[b or 0]), chunk_sums(sums1, c, slice(0, D)),
                                        tiles(h_or_rdeg[:, at(c * CN, CN)]), ALU.mult).then_inc(mean_done, 1)

            def add_root(c, n, b=None):
                dve.wait_ge(l1_mm, n + 1)
                part = l1_fm[:, at(c * CN, CN)]
                nc.vector.tensor_tensor(part, part, l1_ps[b or 0][0:D, :], ALU.add).then_inc(l1_done, 1)

            def batch_stats(c, n, b=None):
                dve.wait_ge(l1_done, n + 1)
                carry_wait()
                nc.vector.bn_stats(bstats[:, at(c, 1), :].rearrange("f c s -> f (c s)"),
                                   l1_fm[:, at(c * CN, CN)]).then_inc(bstat_done, 1)

            def select1(g, buffer):
                wait_past(dve, agg_done[1], g, g - 1)
                nc.vector.tensor_tensor(
                    sel[:, buffer, :].rearrange("p (k n) -> p k n", n=WIN),
                    iota[:, 0:WIN].unsqueeze(1).to_broadcast([LANES, TPG, WIN]),
                    rel[:, at(g * TPG, TPG)].unsqueeze(2).to_broadcast([LANES, TPG, WIN]),
                    ALU.is_equal).then_inc(sel_done[1], 1)

            def group1(j, s):
                g = j * (2 * SLOTS) + s
                if isinstance(g, int) and g == 0:
                    select1(0, 0)
                select1(g + 1, (s + 1) % 2)

            def add_window1(start, width, source, groups_added, units_added):
                window = sums1[:, bass.ds(start, width)]
                wait_past(dve, acc_done[1], groups_added, groups_added)
                wait_past(dve, unit_added, units_added, units_added)
                return nc.vector.tensor_tensor(window, window, source, ALU.add)

            def add_group1(g, units_added):
                start = dve.value_load(base_i[0:1, at(g, 1)], min_val=0, max_val=NODES - 1)
                dve.wait_ge(agg_done[1], g + 1)
                add_window1(start, WIN, agg1_ps[0:D, 0:WIN], g, units_added).then_inc(acc_done[1], 1)

            def hot(tile, buffer):
                wait_past(dve, counted, tile, tile - HOTS + 1)
                nc.vector.tensor_scalar(hot_b[:, buffer, :], iota16[:, 0:LANES], src_b[:, at(tile, 1)], None,
                                        ALU.is_equal)
                nc.vector.tensor_scalar(hot_c[:, buffer, :], iota16[:, :], column[:, at(tile, 1)], None,
                                        ALU.is_equal).then_inc(hot_done, 1)

            def dense(v, b, t, stages, groups_added):
                if "build" in stages:
                    tile = v * TPU + t
                    if isinstance(tile, int) and tile == 0:
                        for n in range(LOOK):
                            hot(n, hot_buffer(b, n))
                    hot(tile + LOOK, hot_buffer(b, t + LOOK))
                if "finish" in stages and t == 1:
                    ps = unit_ps[b][0:UCOLS]
                    wait_past(dve, placed, v, v - 2)
                    nc.vector.tensor_scalar(placer[0:UCOLS, :], iota[0:UCOLS, 0:UWIN],
                                            place[0:UCOLS, at(v - 2, 1)], None,
                                            ALU.is_equal).then_inc(placer_done, 1)
                    dve.wait_ge(unit_hi, v - 1)
                    nc.vector.tensor_tensor(unit_sum[0:UCOLS, 1, :], ps[:, D:2 * D], unit_sum[0:UCOLS, 0, :],
                                            ALU.add).then_inc(unit_mid, 1)
                    dve.wait_ge(unit_mid, v - 1)
                    nc.vector.tensor_tensor(unit_sum[0:UCOLS, 2, :], ps[:, 2 * D:3 * D],
                                            unit_sum[0:UCOLS, 1, :], ALU.add).then_inc(unit_summed, 1)
                if "finish" in stages and t == PLACE_STEP:
                    start = dve.value_load(unit_i[0:1, at(v - 2, 1)], min_val=0, max_val=NODES - 1)
                    dve.wait_ge(placed, v - 1)
                    add_window1(start, UWIN, placed_ps[b], groups_added, v - 2
                                ).then_inc(unit_added, 1)

            def mean_whole(c, n, b=None):
                if b is not None:
                    dve.wait_ge(acc_done[1], GATHER_GROUPS)
                    dve.wait_ge(unit_added, UNITS if c == CHUNKS - 1 else UNITS - 1 if c >= DCHUNK else UNITS - 2)
                mean(c, n, b)

            def split(i):
                if i < PARTS:
                    dve.wait_ge(part_hi, i + 1)
                    nc.vector.tensor_tensor(staged(i), staged(i), blocks_of_h2(i, 0),
                                            ALU.subtract).then_inc(part_rest, 1)
                if i > 0:
                    dve.wait_ge(part_mid, i)
                    nc.vector.tensor_tensor(blocks_of_h2(i - 1, 2), staged(i - 1), blocks_of_h2(i - 1, 1),
                                            ALU.subtract).then_inc(part_lo, 1)

            steps0 = {0: [mix], 2: [residual, h2_stats], 3: [h2_scales],
                      DEGREES: [clamp_degrees, invert_degrees]}
            steps1 = {0: [mean], 2: [add_root, batch_stats]}
            steps1_narrow = {1: [mean_whole], 3: [add_root, batch_stats]}

            def flush(p):
                def of_turn(i):
                    add_group(p, i, SLOTS - 1)
                    dve.wait_ge(acc_done[p], (i + 1) * SLOTS)
                return of_turn

            def all_added(p):
                return lambda: dve.wait_ge(gacc_done[p], GROUPS * GWINS)

            with dve.If(wide < 1):
                turns_with_nodes(dve, group(0), steps0, flush(0))
            with dve.Else():
                turns_then_nodes(dve, group_general(0), steps0, all_added(0))
            dve.wait_ge(r_done, CHUNKS)
            dve.wait_ge(rdeg_done, CHUNKS)
            with dve.If(wide < 1):
                pairs_with_dense(dve, group1, dense, steps1_narrow, add_group1, split)
            with dve.Else():
                turns_then_nodes(dve, group_general(1), steps1, all_added(1))

            dve.wait_ge(bstat_done, CHUNKS)
            nc.vector.bn_aggr(bmv[:, :], bstats[:, :, :].rearrange("f c s -> f (c s)")).then_inc(bmv_done, 1)
            dve.wait_ge(bsd_done, 1)
            in_order(nc.vector.reciprocal(bn[:, 1:2], bn[:, 0:1]))
            in_order(nc.vector.tensor_tensor(bn[:, 2:3], bn[:, 1:2], w[0:D, C_GAMMA:C_GAMMA + 1], ALU.mult))
            in_order(nc.vector.tensor_tensor(bn[:, 3:4], bn[:, 2:3], bmv[:, 0:1], ALU.mult))
            nc.vector.tensor_tensor(bn[:, 4:5], w[0:D, C_BETA:C_BETA + 1], bn[:, 3:4],
                                    ALU.subtract).then_inc(affine_done, 1)
            for c in range(CHUNKS):
                dve.wait_ge(y1_turned, c + 1)
                part = x_nm[:, c * CW:(c + 1) * CW]
                nc.vector.tensor_tensor(part, part, node_ps[c % 4][0:NP, 0:CW], ALU.add).then_inc(out_done, 1)


def kernel(x, src, dst, edge_attr_96, L0_gnn_W_edge, L0_gnn_b_edge, L0_gnn_eps, L0_gnn_W1, L0_gnn_b1,
           L0_gnn_W2, L0_gnn_b2, L1_gnn_Wl, L1_gnn_bl, L1_gnn_Wr, L1_gnn_gamma, L1_gnn_beta):
    import concourse.bacc as bacc
    from concourse.bass_utils import run_bass_kernel_spmd

    f = np.float32
    attr_t = np.zeros((D, EPAD), f)
    attr_t[:, :EDGES] = np.asarray(edge_attr_96).T
    src_pad = np.zeros(EPAD, np.int32)
    src_pad[:EDGES] = np.asarray(src)
    dst_pad = np.full(EPAD, NO_NODE, np.int32)
    dst_pad[:EDGES] = np.asarray(dst)
    first = np.full(GROUPS, 0, np.int32)
    real = -(-EDGES // GE)
    first[:real] = dst_pad[::GE][:real]
    dense_edges = np.arange(DT0 * LANES, (DT0 + DTS + LOOK) * LANES)
    is_edge = dense_edges < EDGES
    dense_src, dense_dst = np.zeros(dense_edges.size, np.int32), np.full(dense_edges.size, NO_NODE, np.int32)
    dense_src[is_edge], dense_dst[is_edge] = src_pad[dense_edges[is_edge]], dst_pad[dense_edges[is_edge]]
    tile_first = dst_pad[np.minimum(dense_edges[::LANES], EDGES - 1)]
    column_first = np.zeros((LANES, UNITS), np.int32)
    column_first[:UCOLS] = np.repeat(tile_first[:DTS].reshape(UNITS, TPU).T, DWIN, axis=0)
    column_first[UCOLS:] = column_first[:1]
    column_offset = (np.arange(LANES, dtype=f) % DWIN).reshape(LANES, 1)
    src_blocks = np.ascontiguousarray(
        src_pad.reshape(2 * TURNS, HALF * TPG, LANES).transpose(0, 2, 1))
    dst_cols = np.ascontiguousarray(dst_pad.reshape(GROUPS * TPG, LANES).T)

    w = np.zeros((D + 1, W_COLS), f)
    for at, mat in ((W_EDGE, L0_gnn_W_edge), (W_1, L0_gnn_W1), (W_2, L0_gnn_W2), (W_L, L1_gnn_Wl),
                    (W_R, L1_gnn_Wr)):
        w[:D, at:at + D] = np.asarray(mat).T
    w[D, W_EDGE:W_EDGE + D] = np.asarray(L0_gnn_b_edge)
    w[D, W_2:W_2 + D] = np.asarray(L0_gnn_b2)
    for at, vec in ((C_B1, L0_gnn_b1), (C_BL, L1_gnn_bl), (C_GAMMA, L1_gnn_gamma), (C_BETA, L1_gnn_beta)):
        w[:D, at] = np.asarray(vec)
    w[:, C_EPS] = np.asarray(L0_gnn_eps)

    arrays = {"x": np.ascontiguousarray(x), "edge_attr_t": attr_t, "src_blocks": src_blocks,
              "dst_cols": dst_cols, "dst_first": first.reshape(1, GROUPS),
              "dense_src": np.ascontiguousarray(dense_src.reshape(-1, LANES).T),
              "dense_dst": np.ascontiguousarray(dense_dst.reshape(-1, LANES).T),
              "tile_first": tile_first.reshape(1, DTS + LOOK), "column_first": column_first,
              "unit_first": np.ascontiguousarray(tile_first[:DTS:TPU]).reshape(1, UNITS),
              "column_offset": column_offset, "weights": w,
              "identity": np.eye(LANES, dtype=f)}
    nc = bacc.Bacc("TRN2", target_bir_lowering=False, num_devices=1)
    aps = [nc.dram_tensor(f"in_{n}", a.shape, mybir.dt.from_np(a.dtype), kind="ExternalInput").ap()
           for n, a in arrays.items()]
    out = nc.dram_tensor("out_0", (NODES, D), F32, kind="ExternalOutput").ap()
    graph_layers(nc, *aps, out)
    r = run_bass_kernel_spmd(nc, [{f"in_{n}": a for n, a in arrays.items()}], core_ids=[0])
    return r.results[0]["out_0"]
```
